# Optimizing a Trainium2 kernel written in Bass

```python
import numpy as np
import jax
import jax.numpy as jnp

def _softmax(x, axis=-1):
    return jax.nn.softmax(x, axis=axis)

def _gelu(x):
    return jax.nn.gelu(x, approximate=True)

def _silu(x):
    return jax.nn.silu(x)

def _sigmoid(x):
    return jax.nn.sigmoid(x)

def _layernorm(x, axis=-1, eps=1e-05):
    m = jnp.mean(x, axis=axis, keepdims=True)
    v = jnp.var(x, axis=axis, keepdims=True)
    return (x - m) / jnp.sqrt(v + eps)

def _scatter_add(tgt, idx, src, axis=0):
    return tgt.at[idx].add(src)

def _segment_sum(src, seg, n):
    return jax.ops.segment_sum(src, seg, n)
kernel_name = 'mk_cond_resid_d2_seqx_r4_96a3a3'

def setup_inputs(seed: int=0):
    np.random.seed(seed)
    _w = jnp.asarray

    def _rec_inputs():
        import jax
        import jax.numpy as jnp
        _rk = jax.random.key(seed)
        x = -0.0002928 + 1 * jax.random.normal(jax.random.fold_in(_rk, 1), (32, 64, 256), jnp.float32)
        _lenS = 64 - jax.random.randint(jax.random.fold_in(_rk, 7), (32,), 0, max(1, 64 // 4) + 1, jnp.int32)
        _lenS2 = 64 - jax.random.randint(jax.random.fold_in(_rk, 8), (32,), 0, max(1, 64 // 4) + 1, jnp.int32)
        cond_256 = -0.106481 + 1.03144 * jax.random.normal(jax.random.fold_in(_rk, 12), (32, 64), jnp.float32)
        _validS = jnp.arange(64)[None, :] < _lenS[:, None]
        _validS2 = jnp.arange(64)[None, :] < _lenS2[:, None]
        _causal = jnp.tril(jnp.ones((64, 64), dtype=bool))
        mask_SxS_bk1 = jnp.broadcast_to(_validS[0:1, :], (64, 64))
        return (x, cond_256, mask_SxS_bk1)
    x, cond_256, mask_SxS_bk1 = _rec_inputs()

    def _L0_cond_setup():
        import jax, jax.numpy as jnp
        import numpy as np
        EPS = 1e-06
        key = jax.random.key(seed)
        ks = jax.random.split(key, 8)
        B, S, E, C = (2, 512, 256, 64)
        x = jax.random.normal(ks[0], (B, S, E), dtype=jnp.float32)
        mask = jnp.triu(jnp.ones((S, S), dtype=bool), k=1)
        conditioning = jax.random.normal(ks[1], (B, C), dtype=jnp.float32)
        sc = 1.0 / np.sqrt(E)
        Wq = jax.random.normal(ks[2], (E, E), dtype=jnp.float32) * sc
        Wk = jax.random.normal(ks[3], (E, E), dtype=jnp.float32) * sc
        Wv = jax.random.normal(ks[4], (E, E), dtype=jnp.float32) * sc
        Wo = jax.random.normal(ks[5], (E, E), dtype=jnp.float32) * sc
        rms_scale = jnp.ones((E,), dtype=jnp.float32)
        Wc = jax.random.normal(ks[6], (2 * E, C), dtype=jnp.float32) * 0.02
        bc = jax.random.normal(ks[7], (2 * E,), dtype=jnp.float32) * 0.02
        return {'x': x, 'mask': mask, 'conditioning': conditioning, 'Wq': Wq, 'Wk': Wk, 'Wv': Wv, 'Wo': Wo, 'rms_scale': rms_scale, 'Wc': Wc, 'bc': bc}
    _L0_cond_all = _L0_cond_setup()
    _L0_cond_in = {k: v for k, v in _L0_cond_all.items() if k in ('Wq', 'Wk', 'Wv', 'Wo', 'rms_scale', 'Wc', 'bc')}
    del _L0_cond_all

    def _L1_cond_setup():
        import jax, jax.numpy as jnp
        import numpy as np
        D_MODEL = 256
        D_T = 64
        N_HEADS = 16
        HIDDEN = 4 * D_MODEL
        EPS = 1e-06

        def _tc_rmsnorm(x, t, gw, gb, bw, bb):
            g = (t @ gw.T + gb)[:, None, :]
            b = (t @ bw.T + bb)[:, None, :]
            inv_rms = jax.lax.rsqrt(jnp.mean(x * x, axis=-1, keepdims=True) + EPS)
            return g * x * inv_rms + b

        def _attention(x, Wq, Wk, Wv, Wo):
            B, L, D = x.shape
            H = N_HEADS
            dh = D // H
            scale = np.sqrt(dh).astype(np.float32)
            q = (x @ Wq.T).reshape(B, L, H, dh)
            k = (x @ Wk.T).reshape(B, L, H, dh)
            v = (x @ Wv.T).reshape(B, L, H, dh)
            attn = jnp.einsum('blhd,bmhd->bhlm', q, k) / scale
            p = jax.nn.softmax(attn, axis=-1)
            o = jnp.einsum('bhlm,bmhd->blhd', p, v).reshape(B, L, D)
            return o @ Wo.T

        def _swiglu(x, gate_w, hid_w, out_w):
            return jax.nn.silu(x @ gate_w.T) * (x @ hid_w.T) @ out_w.T
        key = jax.random.key(seed)
        ks = jax.random.split(key, 20)
        B, L = (8, 256)
        s_d = 1.0 / np.sqrt(D_MODEL)
        s_t = 1.0 / np.sqrt(D_T)
        s_h = 1.0 / np.sqrt(HIDDEN)
        return {'x': jax.random.normal(ks[0], (B, L, D_MODEL), jnp.float32), 't': jax.random.normal(ks[1], (B, D_T), jnp.float32), 'Wq': jax.random.normal(ks[2], (D_MODEL, D_MODEL), jnp.float32) * s_d, 'Wk': jax.random.normal(ks[3], (D_MODEL, D_MODEL), jnp.float32) * s_d, 'Wv': jax.random.normal(ks[4], (D_MODEL, D_MODEL), jnp.float32) * s_d, 'Wo': jax.random.normal(ks[5], (D_MODEL, D_MODEL), jnp.float32) * s_d, 'g1w': jax.random.normal(ks[6], (D_MODEL, D_T), jnp.float32) * s_t, 'g1b': jnp.ones((D_MODEL,), jnp.float32), 'b1w': jax.random.normal(ks[7], (D_MODEL, D_T), jnp.float32) * s_t, 'b1b': jnp.zeros((D_MODEL,), jnp.float32), 'g2w': jax.random.normal(ks[8], (D_MODEL, D_T), jnp.float32) * s_t, 'g2b': jnp.ones((D_MODEL,), jnp.float32), 'b2w': jax.random.normal(ks[9], (D_MODEL, D_T), jnp.float32) * s_t, 'b2b': jnp.zeros((D_MODEL,), jnp.float32), 'gate_w': jax.random.normal(ks[10], (HIDDEN, D_MODEL), jnp.float32) * s_d, 'hid_w': jax.random.normal(ks[11], (HIDDEN, D_MODEL), jnp.float32) * s_d, 'out_w': jax.random.normal(ks[12], (D_MODEL, HIDDEN), jnp.float32) * s_h}
    _L1_cond_all = _L1_cond_setup()
    _L1_cond_in = {k: v for k, v in _L1_cond_all.items() if k in ('Wq', 'Wk', 'Wv', 'Wo', 'g1w', 'g1b', 'b1w', 'b1b', 'g2w', 'g2b', 'b2w', 'b2b', 'gate_w', 'hid_w', 'out_w')}
    del _L1_cond_all
    return {'x': x, 'cond_256': cond_256, 'mask_SxS_bk1': mask_SxS_bk1, 'L0_cond_Wq': _L0_cond_in['Wq'], 'L0_cond_Wk': _L0_cond_in['Wk'], 'L0_cond_Wv': _L0_cond_in['Wv'], 'L0_cond_Wo': _L0_cond_in['Wo'], 'L0_cond_rms_scale': _L0_cond_in['rms_scale'], 'L0_cond_Wc': _L0_cond_in['Wc'], 'L0_cond_bc': _L0_cond_in['bc'], 'L1_cond_Wq': _L1_cond_in['Wq'], 'L1_cond_Wk': _L1_cond_in['Wk'], 'L1_cond_Wv': _L1_cond_in['Wv'], 'L1_cond_Wo': _L1_cond_in['Wo'], 'L1_cond_g1w': _L1_cond_in['g1w'], 'L1_cond_g1b': _L1_cond_in['g1b'], 'L1_cond_b1w': _L1_cond_in['b1w'], 'L1_cond_b1b': _L1_cond_in['b1b'], 'L1_cond_g2w': _L1_cond_in['g2w'], 'L1_cond_g2b': _L1_cond_in['g2b'], 'L1_cond_b2w': _L1_cond_in['b2w'], 'L1_cond_b2b': _L1_cond_in['b2b'], 'L1_cond_gate_w': _L1_cond_in['gate_w'], 'L1_cond_hid_w': _L1_cond_in['hid_w'], 'L1_cond_out_w': _L1_cond_in['out_w']}

def reference(x, cond_256, mask_SxS_bk1, L0_cond_Wq, L0_cond_Wk, L0_cond_Wv, L0_cond_Wo, L0_cond_rms_scale, L0_cond_Wc, L0_cond_bc, L1_cond_Wq, L1_cond_Wk, L1_cond_Wv, L1_cond_Wo, L1_cond_g1w, L1_cond_g1b, L1_cond_b1w, L1_cond_b1b, L1_cond_g2w, L1_cond_g2b, L1_cond_b2w, L1_cond_b2b, L1_cond_gate_w, L1_cond_hid_w, L1_cond_out_w):
    import jax
    import jax.numpy as jnp

    def _L0_cond_ref(x, mask, conditioning, Wq, Wk, Wv, Wo, rms_scale, Wc, bc):
        import jax, jax.numpy as jnp
        import numpy as np
        EPS = 1e-06
        B, S, E = x.shape
        H = 16
        D = E // H
        scale = D ** (-0.5)

        def proj(W):
            return (x @ W.T).reshape(B, S, H, D).transpose(0, 2, 1, 3)
        q, k, v = (proj(Wq), proj(Wk), proj(Wv))
        scores = jnp.einsum('bhsd,bhtd->bhst', q, k) * scale
        scores = jnp.where(mask[None, None, :, :], -jnp.inf, scores)
        attn = jax.nn.softmax(scores, axis=-1)
        out = jnp.einsum('bhst,bhtd->bhsd', attn, v)
        out = out.transpose(0, 2, 1, 3).reshape(B, S, E)
        out = out @ Wo.T
        rms = jnp.sqrt(jnp.mean(out * out, axis=-1, keepdims=True) + EPS)
        xn = out / rms * rms_scale
        mod = jax.nn.silu(conditioning) @ Wc.T + bc
        shift, sc = jnp.split(mod, 2, axis=-1)
        xn = xn * (1.0 + sc[:, None, :]) + shift[:, None, :]
        return xn

    def _L1_cond_ref(x, t, Wq, Wk, Wv, Wo, g1w, g1b, b1w, b1b, g2w, g2b, b2w, b2b, gate_w, hid_w, out_w):
        import jax, jax.numpy as jnp
        import numpy as np
        D_MODEL = 256
        D_T = 64
        N_HEADS = 16
        HIDDEN = 4 * D_MODEL
        EPS = 1e-06

        def _tc_rmsnorm(x, t, gw, gb, bw, bb):
            g = (t @ gw.T + gb)[:, None, :]
            b = (t @ bw.T + bb)[:, None, :]
            inv_rms = jax.lax.rsqrt(jnp.mean(x * x, axis=-1, keepdims=True) + EPS)
            return g * x * inv_rms + b

        def _attention(x, Wq, Wk, Wv, Wo):
            B, L, D = x.shape
            H = N_HEADS
            dh = D // H
            scale = np.sqrt(dh).astype(np.float32)
            q = (x @ Wq.T).reshape(B, L, H, dh)
            k = (x @ Wk.T).reshape(B, L, H, dh)
            v = (x @ Wv.T).reshape(B, L, H, dh)
            attn = jnp.einsum('blhd,bmhd->bhlm', q, k) / scale
            p = jax.nn.softmax(attn, axis=-1)
            o = jnp.einsum('bhlm,bmhd->blhd', p, v).reshape(B, L, D)
            return o @ Wo.T

        def _swiglu(x, gate_w, hid_w, out_w):
            return jax.nn.silu(x @ gate_w.T) * (x @ hid_w.T) @ out_w.T
        x = x + _attention(_tc_rmsnorm(x, t, g1w, g1b, b1w, b1b), Wq, Wk, Wv, Wo)
        return x + _swiglu(_tc_rmsnorm(x, t, g2w, g2b, b2w, b2b), gate_w, hid_w, out_w)
    x = x + _L0_cond_ref(x, mask_SxS_bk1, cond_256, L0_cond_Wq, L0_cond_Wk, L0_cond_Wv, L0_cond_Wo, L0_cond_rms_scale, L0_cond_Wc, L0_cond_bc)
    x = x + _L1_cond_ref(x, cond_256, L1_cond_Wq, L1_cond_Wk, L1_cond_Wv, L1_cond_Wo, L1_cond_g1w, L1_cond_g1b, L1_cond_b1w, L1_cond_b1b, L1_cond_g2w, L1_cond_g2b, L1_cond_b2w, L1_cond_b2b, L1_cond_gate_w, L1_cond_hid_w, L1_cond_out_w)
    return x

_drawn_inputs = setup_inputs


def setup_inputs(seed=0):
    import zlib

    import numpy as np

    out = dict(_drawn_inputs(seed))
    spreads = {'L0_cond_rms_scale': (1.0, 0.2),
     'L1_cond_g1b': (1.0, 0.2),
     'L1_cond_b1b': (0.0, 0.1),
     'L1_cond_g2b': (1.0, 0.2),
     'L1_cond_b2b': (0.0, 0.1)}
    factors = {'L0_cond_bc': 2.69}
    for name, (base, spread) in spreads.items():
        noise = np.random.default_rng([zlib.crc32(name.encode()), seed]).standard_normal(out[name].shape)
        drawn = base * np.exp(spread * noise) if base else spread * noise
        out[name] = jnp.asarray(drawn.astype(out[name].dtype))
    for name, factor in factors.items():
        out[name] = (out[name] * factor).astype(out[name].dtype)
    return out
```

```python
from contextlib import ExitStack

import concourse.bass as bass
from concourse import mybir

ALU = mybir.AluOpType
ACT = mybir.ActivationFunctionType
AXX = mybir.AxisListType.X
F32 = mybir.dt.float32
F32R = mybir.dt.float32r
I32 = mybir.dt.int32
U8 = mybir.dt.uint8

P = 128
NB, S, D = 32, 64, 256
H, DH = 16, 16
DT = 64
HID = 1024
KT = D // P
HH = H // KT
NP = H // 2
DE = DH + 1
NT = 2
TC = NT * P
NCH = NB * S // TC
CB = TC // S
NI = NT * KT
NJ = HID // P
EPS = 1e-6
SCALE = DH ** -0.5
BIG = 1e30
NEWTON = 3
CHAIN = 3 + 3 * NEWTON
ROOT_SEED = 0x5F3759DF

WCOL = {w: 512 * n for n, w in enumerate(["k0", "q0", "v0", "o0", "k1", "q1", "v1", "o1"])}
WCOL["gate"], WCOL["hid"], WCOL["out"] = 4096, 4096 + 2 * HID, 4096 + 4 * HID
WBLK = 512
NWB = (4096 + 6 * HID) // WBLK
NSTAGE = 3

GU = (0, 1)
ACC = 2
SC, PT = 3, 4
OB = (5, 6)
QB, KB, VB = 6, 7, 5
OTB, YB = 7, 5
XTB = (6, 0)


def wait(eng, s, count):
    if not (isinstance(count, int) and count <= 0):
        eng.wait_ge(s, count)


def build(nc, a, out):
    ctx = ExitStack()
    with ctx:
        def sb(name, shape, dt=F32):
            return ctx.enter_context(nc.sbuf_tensor(name, shape, dt))

        def sem(name):
            return ctx.enter_context(nc.semaphore(name))

        ps = ctx.enter_context(nc.psum_tensor("ps", [P, 8, 512], F32))
        mod_dram = nc.dram_tensor("mod_rows_dram", [NB, 2 * D], F32, kind="Internal").ap()

        w_stage = sb("w_stage", [P, NSTAGE, WBLK])
        w_hi = sb("w_hi", [P, NWB * WBLK], F32R)
        w_lo = sb("w_lo", [P, NWB * WBLK], F32R)
        ident = sb("ident", [P, P])
        seq_sel = sb("seq_sel", [S, P], F32R)
        mask_u8 = sb("mask_u8", [S, S], U8)
        mask_neg = sb("mask_neg", [S, HH, S], F32R)
        condT = sb("condT", [DT, NB])
        condT_silu = sb("condT_silu", [DT, NB])
        wcT = sb("wcT", [DT, 2 * D])
        bc_rows = sb("bc_rows", [NB, 2 * D])
        rms_rows = sb("rms_rows", [NB, D])
        mod_rows = sb("mod_rows", [NB, 2 * D])
        modw = sb("modw", [DT, 4, D])
        modb = sb("modb", [P, 4 * KT])
        modT = sb("modT", [P, 4, KT, NB])

        x_T = sb("x_T", [P, KT, TC])
        x_row = sb("x_row", [P, NT, D])
        in_hi = sb("in_hi", [P, KT, TC], F32R)
        in_lo = sb("in_lo", [P, KT, TC], F32R)
        ff_hi = sb("ff_hi", [P, KT, TC], F32R)
        ff_lo = sb("ff_lo", [P, KT, TC], F32R)
        q_T = sb("q_T", [P, KT, TC])
        k_T = sb("k_T", [P, KT, TC])
        k_diag = sb("k_diag", [P, KT, HH, TC])
        v_pairs = sb("v_pairs", [P, NT, 2, NP, 2 * DE])
        row_max = sb("row_max", [P, HH])
        shifted = sb("shifted", [P, 2, HH * S])
        probs = sb("probs", [P, 2, HH * S])
        probs_T = sb("probs_T", [P, 2, 4 * P])
        inv_sum = sb("inv_sum", [P, H])
        o_row = sb("o_row", [P, NT, D])
        o_hi = sb("o_hi", [P, NT, KT, P], F32R)
        o_lo = sb("o_lo", [P, NT, KT, P], F32R)
        mod_tile = sb("mod_tile", [P, NT, 2 * D])
        x_shift = sb("x_shift", [P, NT, D])
        y_mod = sb("y_mod", [P, NT, D])
        x1 = sb("x1", [P, NT, D])
        x2 = sb("x2", [P, NT, D])
        sq_junk = sb("sq_junk", [P, NT, D])
        sumsq = sb("sumsq", [P, 3, NT])
        mean_sq = sb("mean_sq", [P, NT])
        root_bits = sb("root_bits", [P, NT], I32)
        root = sb("root", [P, 3, NT])
        root_i = sb("root_i", [P, NT], I32)
        root_a = sb("root_a", [P, NT])
        root_b = sb("root_b", [P, NT])
        xs_row = [sb(f"xs_row{n}", [P, NT, D]) for n in range(2)]
        xs_g = [sb(f"xs_g{n}", [P, KT, TC]) for n in range(2)]
        xs_gb = [sb(f"xs_gb{n}", [P, KT, TC]) for n in range(2)]
        gate_t = sb("gate_t", [P, 2, TC])
        gate_s = sb("gate_s", [P, TC])
        h_T = sb("h_T", [P, 2, TC])
        h_hi = sb("h_hi", [P, 2, TC], F32R)
        h_lo = sb("h_lo", [P, 2, TC], F32R)
        res_sum = sb("res_sum", [P, NT, D])
        res = sb("res", [P, NT, D])

        w_landed = [sem(f"w_landed{n}") for n in range(NSTAGE)]
        w_hi_done, w_lo_done = sem("w_hi_done"), sem("w_lo_done")
        consts_landed, pool_set = sem("consts_landed"), sem("pool_set")
        ident_ready, v_ones_set = sem("ident_ready"), sem("v_ones_set")
        sel_ready, mask_ready = sem("sel_ready"), sem("mask_ready")
        silu_ready, mod_ready = sem("silu_ready"), sem("mod_ready")
        mod_chain, modT_done, mod_stored = sem("mod_chain"), sem("modT_done"), sem("mod_stored")
        xT_landed, xrow_landed, modtile_landed = sem("xT_landed"), sem("xrow_landed"), sem("modtile_landed")
        kdiag_landed, res_stored = sem("kdiag_landed"), sem("res_stored")
        in_hi_ready, in_lo_ready = sem("in_hi_ready"), sem("in_lo_ready")
        k_ready, q_ready, v_ready = sem("k_ready"), sem("q_ready"), sem("v_ready")
        k_copied, q_copied, v_copied = sem("k_copied"), sem("q_copied"), sem("v_copied")
        scores_ready, max_ready, max_clamped = sem("scores_ready"), sem("max_ready"), sem("max_clamped")
        shifted_ready, probs_ready = sem("shifted_ready"), sem("probs_ready")
        pT_ready, pT_copied = sem("pT_ready"), sem("pT_copied")
        pv_ready, inv_ready, o_ready = sem("pv_ready"), sem("inv_ready"), sem("o_ready")
        oT_ready, o_hi_ready, o_lo_ready = sem("oT_ready"), sem("o_hi_ready"), sem("o_lo_ready")
        y_ready = sem("y_ready")
        y_squared, x_squared, newton = sem("y_squared"), sem("x_squared"), sem("newton")
        shift_ready, y_mod_ready = sem("shift_ready"), sem("y_mod_ready")
        x1_ready, x2_ready, res_sum_ready = sem("x1_ready"), sem("x2_ready"), sem("res_sum_ready")
        xs_ready = [sem(f"xs_ready{n}") for n in range(2)]
        xsT_ready = [sem(f"xsT_ready{n}") for n in range(2)]
        xs_g_ready = [sem(f"xs_g_ready{n}") for n in range(2)]
        xs_gb_ready = [sem(f"xs_gb_ready{n}") for n in range(2)]
        ff_hi_ready, ff_lo_ready = sem("ff_hi_ready"), sem("ff_lo_ready")
        gu_ready, tanh_ready, gate_ready = sem("gu_ready"), sem("tanh_ready"), sem("gate_ready")
        h_ready, h_hi_ready, h_lo_ready = sem("h_ready"), sem("h_hi_ready"), sem("h_lo_ready")
        acc_ready, res_ready = sem("acc_ready"), sem("res_ready")

        block = ctx.enter_context(nc.Block())

        CONSTS = (
            (condT[:], a["condT"]), (wcT[:], a["wcT"]), (mask_u8[:], a["mask"]),
            (bc_rows[:], a["bc"].partition_broadcast(NB)),
            (rms_rows[:], a["rms"].partition_broadcast(NB)),
            (modw[:, 0, :], a["g1wT"]), (modw[:, 1, :], a["b1wT"]),
            (modw[:, 2, :], a["g2wT"]), (modw[:, 3, :], a["b2wT"]),
            (modb[:], a["modb"]),
        )

        def by_seq(t):
            return t.rearrange("p k (b s) -> p k b s", s=S)

        def mod_of(which, c):
            return modT[:, which, :, bass.ds(c * CB, CB)].unsqueeze(3).to_broadcast([P, KT, CB, S])

        def w_parts(name, k, c0, n, width=D):
            at = WCOL[name] + k * width + c0
            return w_hi[:, at:at + n], w_lo[:, at:at + n]

        @block.sync
        def _(sp):
            def load_w(n):
                wait(sp, w_hi_done, n - NSTAGE + 1)
                wait(sp, w_lo_done, n - NSTAGE + 1)
                sp.dma_start(w_stage[:, n % NSTAGE, :], a["weights"][:, n * WBLK:(n + 1) * WBLK])\
                    .then_inc(w_landed[n % NSTAGE], 16)

            for n in range(NSTAGE):
                load_w(n)
            for dst, src in CONSTS:
                sp.dma_start(dst, src).then_inc(consts_landed, 16)
            for n in range(NSTAGE, NWB):
                load_w(n)

            def loads(c):
                wait(sp, in_lo_ready, 2 * c - 1)
                sp.dma_start(x_T[:], a["xT"][bass.ds(c, 1)].rearrange("a p k s -> (a p) k s"))\
                    .then_inc(xT_landed, 16)
                wait(sp, shift_ready, c)
                sp.dma_start(x_row[:], a["x"][bass.ds(c, 1)].rearrange("a t p f -> (a p) t f"))\
                    .then_inc(xrow_landed, 16)
                wait(sp, y_mod_ready, c)
                for b in range(CB):
                    sp.dma_start(mod_tile[S * (b % 2):S * (b % 2) + S, b // 2, :],
                                 mod_dram[bass.ds(c * CB + b, 1)].rearrange("a n -> (a n)")
                                 .partition_broadcast(S)).then_inc(modtile_landed, 16)

            def keys(c, l):
                sp.wait_ge(k_copied, 2 * c + l + 1)
                for h in range(HH):
                    rows = slice(DH * h, DH * h + DH)
                    sp.dma_start(k_diag[rows, :, h, :], k_T[rows, :, :]).then_inc(kdiag_landed, 16)

            def store(f):
                sp.wait_ge(res_ready, f + 1)
                sp.dma_start(out[bass.ds(f, 1)].rearrange("a t p f -> (a p) t f"), res[:])\
                    .then_inc(res_stored, 16)

            def turn(c):
                loads(c)
                keys(c, 0)
                keys(c, 1)

            sp.wait_ge(mod_stored, 16)
            turn(0)
            turn(1)
            store(0)
            with sp.Fori(2, NCH) as c:
                turn(c)
                store(c - 1)
            store(NCH - 1)
            sp.wait_ge(res_stored, 16 * NCH)

        @block.gpsimd
        def _(pool):
            pool.memset(ident[:], 0.0).then_inc(pool_set, 1)
            pool.memset(k_diag[:], 0.0).then_inc(pool_set, 1)
            pool.memset(v_pairs[:], 0.0).then_inc(pool_set, 1)
            pool.wait_ge(pool_set, 3)
            pool.affine_select(out=ident[:], in_=ident[:], compare_op=ALU.not_equal, fill=1.0,
                               base=0, pattern=[[-1, P]], channel_multiplier=1).then_inc(ident_ready, 1)
            pool.wait_ge(ident_ready, 1)
            pool.memset(v_pairs[0:S, :, :, :, DH:DE], 1.0).then_inc(v_ones_set, 1)
            pool.wait_ge(v_ones_set, 1)
            pool.memset(v_pairs[S:P, :, :, :, DE + DH:2 * DE], 1.0).then_inc(v_ones_set, 1)
            pool.wait_ge(v_ones_set, 2)
            pool.wait_ge(mod_chain, 3)
            pool.dma_start(mod_dram, mod_rows[:]).then_inc(mod_stored, 16)

            def shift_in(c):
                pool.wait_ge(xrow_landed, 16 * (c + 1))
                pool.wait_ge(modtile_landed, 16 * CB * (c + 1))
                wait(pool, x1_ready, c)
                pool.tensor_tensor(x_shift[:], x_row[:], mod_tile[:, :, D:2 * D], ALU.add)\
                    .then_inc(shift_ready, 1)

            def new_x1(c):
                pool.wait_ge(y_mod_ready, c + 1)
                pool.wait_ge(shift_ready, c + 1)
                wait(pool, res_sum_ready, c)
                wait(pool, xs_ready[0], c)
                pool.tensor_tensor(x1[:], y_mod[:], x_shift[:], ALU.add).then_inc(x1_ready, 1)

            def bias_in(n, c):
                pool.wait_ge(xs_g_ready[n], c + 1)
                wait(pool, in_hi_ready if n == 0 else ff_hi_ready, 2 * c if n == 0 else c)
                pool.tensor_tensor(by_seq(xs_gb[n][:]), by_seq(xs_g[n][:]), mod_of(2 * n + 1, c),
                                   ALU.add).then_inc(xs_gb_ready[n], 1)

            def sum_residuals(c):
                pool.wait_ge(x2_ready, c + 1)
                wait(pool, res_ready, c)
                pool.tensor_tensor(res_sum[:], x1[:], x2[:], ALU.add).then_inc(res_sum_ready, 1)

            def hidden_lo(f, j):
                pool.wait_ge(h_hi_ready, NJ * f + j + 1)
                pool.tensor_tensor(h_lo[:, j % 2, :], h_T[:, j % 2, :], h_hi[:, j % 2, :],
                                   ALU.subtract).then_inc(h_lo_ready, 1)

            def turn(c, f):
                if f is not None:
                    bias_in(1, f)
                if c is not None:
                    shift_in(c)
                for j in range(4):
                    if f is not None:
                        hidden_lo(f, j)
                if c is not None:
                    new_x1(c)
                for j in range(4, 7):
                    if f is not None:
                        hidden_lo(f, j)
                if c is not None:
                    bias_in(0, c)
                if f is not None:
                    hidden_lo(f, 7)
                if c is not None:
                    sum_residuals(c)

            pool.wait_ge(modT_done, 1)
            turn(0, None)
            turn(1, 0)
            with pool.Fori(2, NCH) as c:
                turn(c, c - 1)
            turn(None, NCH - 1)

        @block.scalar
        def _(act):
            act.wait_ge(consts_landed, 16 * len(CONSTS))
            act.activation(condT_silu[:], condT[:], ACT.Silu).then_inc(silu_ready, 1)
            for n in range(NWB):
                act.wait_ge(w_landed[n % NSTAGE], 16 * (n // NSTAGE + 1))
                act.activation(w_hi[:, n * WBLK:(n + 1) * WBLK], w_stage[:, n % NSTAGE, :], ACT.Copy)\
                    .then_inc(w_hi_done, 1)

            def input_hi(c, l):
                if l == 0:
                    act.wait_ge(xT_landed, 16 * (c + 1))
                    wait(act, v_ready, 2 * c)
                    wait(act, in_lo_ready, 2 * c)
                else:
                    act.wait_ge(xs_gb_ready[0], c + 1)
                act.activation(in_hi[:], (x_T if l == 0 else xs_gb[0])[:], ACT.Copy)\
                    .then_inc(in_hi_ready, 1)

            def ff_input_hi(f):
                act.wait_ge(xs_gb_ready[1], f + 1)
                act.activation(ff_hi[:], xs_gb[1][:], ACT.Copy).then_inc(ff_hi_ready, 1)

            def copy_kq(c, l):
                act.wait_ge(k_ready, 2 * c + l + 1)
                wait(act, kdiag_landed, 16 * HH * (2 * c + l))
                act.activation(k_T[:], ps[:, KB, :], ACT.Copy).then_inc(k_copied, 1)
                act.wait_ge(q_ready, 2 * c + l + 1)
                act.activation(q_T[:], ps[:, QB, :], ACT.Copy).then_inc(q_copied, 1)

            def exponentials(c, l, i):
                n = NI * (2 * c + l) + i
                act.wait_ge(shifted_ready, n + 1)
                wait(act, pT_ready, n - 1)
                act.activation(probs[:, i % 2, :], shifted[:, i % 2, :], ACT.Exp, scale=SCALE)\
                    .then_inc(probs_ready, 1)

            def copy_pT(c, l, i):
                n = NI * (2 * c + l) + i
                act.wait_ge(pT_ready, n + 1)
                wait(act, pv_ready, n - 1)
                act.activation(probs_T[:, i % 2, :], ps[:, PT, :], ACT.Copy).then_inc(pT_copied, 1)

            def output_hi(c, l):
                act.wait_ge(oT_ready, 2 * c + l + 1)
                wait(act, y_ready, 2 * c + l)
                act.activation(o_hi[:], ps[:, OTB, :], ACT.Copy).then_inc(o_hi_ready, 1)

            def squares(src, n, waits, done):
                for s, count in waits:
                    wait(act, s, count)
                for t in range(NT):
                    ins = act.activation(sq_junk[:, t, :], src(t), ACT.Square,
                                         accum_out=sumsq[:, n, t:t + 1])
                ins.then_inc(done, 1)

            def tanh(f, j):
                act.wait_ge(gu_ready, NJ * f + j + 1)
                wait(act, gate_ready, NJ * f + max(j - 1, 0))
                act.activation(gate_t[:, j % 2, :], ps[:, GU[j % 2], 0:TC], ACT.Tanh, scale=0.5)\
                    .then_inc(tanh_ready, 1)

            def hidden_hi(f, j):
                act.wait_ge(h_ready, NJ * f + j + 1)
                act.activation(h_hi[:, j % 2, :], h_T[:, j % 2, :], ACT.Copy).then_inc(h_hi_ready, 1)

            def hidden(f, j):
                if f is not None:
                    tanh(f, j)
                    hidden_hi(f, j)

            def attention(c, l, f):
                j = 7 * l
                exponentials(c, l, 0)
                hidden(f, j)
                copy_pT(c, l, 0)
                exponentials(c, l, 1)
                copy_pT(c, l, 1)
                exponentials(c, l, 2)
                copy_pT(c, l, 2)
                exponentials(c, l, 3)
                if l == 0:
                    hidden(f, 1)
                copy_pT(c, l, 3)
                if l == 0:
                    hidden(f, 2)
                output_hi(c, l)

            def turn(c, f):
                if c is not None:
                    input_hi(c, 0)
                    copy_kq(c, 0)
                if f is not None:
                    ff_input_hi(f)
                if c is None:
                    for j in range(NJ):
                        hidden(f, j)
                    return
                attention(c, 0, f)
                hidden(f, 3)
                squares(lambda t: ps[:, YB, D * t:D * t + D], 0,
                        [(y_ready, 2 * c + 1), (x_squared, 2 * c)], y_squared)
                hidden(f, 4)
                hidden(f, 5)
                squares(lambda t: x1[:, t, :], 1, [(x1_ready, c + 1), (y_squared, c + 1)], x_squared)
                hidden(f, 6)
                input_hi(c, 1)
                copy_kq(c, 1)
                attention(c, 1, f)
                squares(lambda t: x2[:, t, :], 2, [(x2_ready, c + 1), (x_squared, 2 * c + 1)], x_squared)

            turn(0, None)
            turn(1, 0)
            with act.Fori(2, NCH) as c:
                turn(c, c - 1)
            turn(None, NCH - 1)

        @block.vector
        def _(dve):
            dve.wait_ge(consts_landed, 16 * len(CONSTS))
            dve.tensor_scalar(mask_neg[:], mask_u8[:].unsqueeze(1).to_broadcast([S, HH, S]), -BIG,
                              None, ALU.mult).then_inc(mask_ready, 1)
            dve.wait_ge(ident_ready, 1)
            dve.tensor_copy(seq_sel[:].rearrange("q (a r) -> q a r", a=2),
                            ident[0:S, 0:S].unsqueeze(1).to_broadcast([S, 2, S])).then_inc(sel_ready, 1)
            dve.wait_ge(mod_ready, 1)
            dve.tensor_tensor(mod_rows[:, D:2 * D], ps[0:NB, 0, 0:D], bc_rows[:, 0:D], ALU.add)\
                .then_inc(mod_chain, 1)
            dve.tensor_tensor(mod_rows[:, 0:D], ps[0:NB, 0, D:2 * D], bc_rows[:, D:2 * D], ALU.add)\
                .then_inc(mod_chain, 1)
            dve.wait_ge(mod_chain, 2)
            dve.scalar_tensor_tensor(out=mod_rows[:, 0:D], in0=mod_rows[:, 0:D], scalar=1.0,
                                     in1=rms_rows[:], op0=ALU.add, op1=ALU.mult).then_inc(mod_chain, 1)
            dve.wait_ge(mod_ready, 2)
            dve.tensor_tensor(modT[:].rearrange("p w k b -> p (w k) b"),
                              ps[:, 1, 0:4 * KT * NB].rearrange("p (i b) -> p i b", b=NB),
                              modb[:].unsqueeze(2).to_broadcast([P, 4 * KT, NB]), ALU.add)\
                .then_inc(modT_done, 1)
            for n in range(NWB):
                dve.wait_ge(w_hi_done, n + 1)
                dve.tensor_tensor(w_lo[:, n * WBLK:(n + 1) * WBLK], w_stage[:, n % NSTAGE, :],
                                  w_hi[:, n * WBLK:(n + 1) * WBLK], ALU.subtract).then_inc(w_lo_done, 1)
            dve.wait_ge(modT_done, 1)
            dve.wait_ge(v_ones_set, 2)

            def input_lo(c, l):
                dve.wait_ge(in_hi_ready, 2 * c + l + 1)
                dve.tensor_tensor(in_lo[:], (x_T if l == 0 else xs_gb[0])[:], in_hi[:], ALU.subtract)\
                    .then_inc(in_lo_ready, 1)

            def values(c, l):
                dve.wait_ge(v_ready, 2 * c + l + 1)
                for par in range(2):
                    for b in range(2):
                        ins = dve.tensor_copy(
                            v_pairs[S * par:S * par + S, :, b, :, DE * par:DE * par + DH],
                            ps[S * b:S * b + S, VB, :].rearrange("p (t j e d) -> p t j e d",
                                                                  t=NT, j=NP, e=2)[:, :, :, par, :])
                ins.then_inc(v_copied, 1)

            def shift_scores(c, l, i):
                n = NI * (2 * c + l) + i
                scores = ps[:, SC, :].rearrange("p (h s) -> p h s", s=S)
                dve.wait_ge(scores_ready, n + 1)
                wait(dve, shifted_ready, n)
                dve.tensor_reduce(row_max[:], scores, AXX, ALU.max).then_inc(max_ready, 1)
                dve.wait_ge(max_ready, n + 1)
                if l == 0:
                    dve.tensor_scalar(row_max[:], row_max[:], -BIG / 2, None, ALU.max)\
                        .then_inc(max_clamped, 1)
                    dve.wait_ge(max_clamped, NI * c + i + 1)
                wait(dve, probs_ready, n - 1)
                dve.tensor_tensor(shifted[:, i % 2, :].rearrange("p (h s) -> p h s", s=S), scores,
                                  row_max[:].unsqueeze(2).to_broadcast([P, HH, S]), ALU.subtract)\
                    .then_inc(shifted_ready, 1)

            def norm_output(c, l, t):
                n = NT * (2 * c + l) + t
                sums = ps[:, OB[t], 0:H * DE].rearrange("p (h e) -> p h e", e=DE)
                dve.wait_ge(pv_ready, NI * (2 * c + l) + KT * t + KT)
                wait(dve, o_ready, n)
                wait(dve, oT_ready, 2 * c + l)
                dve.reciprocal(inv_sum[:], sums[:, :, DH]).then_inc(inv_ready, 1)
                dve.wait_ge(inv_ready, n + 1)
                dve.tensor_tensor(o_row[:, t, :].rearrange("p (h d) -> p h d", d=DH), sums[:, :, 0:DH],
                                  inv_sum[:].unsqueeze(2).to_broadcast([P, H, DH]), ALU.mult)\
                    .then_inc(o_ready, 1)

            def output_lo(c, l):
                dve.wait_ge(o_hi_ready, 2 * c + l + 1)
                dve.tensor_tensor(o_lo[:].rearrange("p t k s -> p (t k s)"), ps[:, OTB, :],
                                  o_hi[:].rearrange("p t k s -> p (t k s)"), ALU.subtract)\
                    .then_inc(o_lo_ready, 1)

            def inverse_root(c, r, done, count):
                at = [CHAIN * (3 * c + r)]

                def link(ins):
                    at[0] = at[0] + 1
                    ins.then_inc(newton, 1)
                    dve.wait_ge(newton, at[0])

                y = root[:, r, :]
                dve.wait_ge(done, count)
                link(dve.tensor_scalar(mean_sq[:], sumsq[:, r, :], 1.0 / D, EPS, ALU.mult, ALU.add))
                link(dve.tensor_scalar(root_bits[:], mean_sq[:].bitcast(I32), 1, None,
                                       ALU.logical_shift_right))
                link(dve.tensor_scalar(root_i[:], root_bits[:], -1, ROOT_SEED, ALU.mult, ALU.add))
                for k in range(NEWTON):
                    y0 = root_i[:].bitcast(F32) if k == 0 else y
                    link(dve.tensor_tensor(root_a[:], y0, y0, ALU.mult))
                    link(dve.scalar_tensor_tensor(out=root_b[:], in0=root_a[:], scalar=-0.5, in1=mean_sq[:],
                                                  op0=ALU.mult, op1=ALU.mult))
                    link(dve.scalar_tensor_tensor(out=y, in0=root_b[:], scalar=1.5, in1=y0,
                                                  op0=ALU.add, op1=ALU.mult))

            def modulate_y(c):
                inverse_root(c, 0, y_squared, c + 1)
                dve.wait_ge(modtile_landed, 16 * CB * (c + 1))
                wait(dve, x1_ready, c)
                for t in range(NT):
                    ins = dve.scalar_tensor_tensor(out=y_mod[:, t, :], in0=ps[:, YB, D * t:D * t + D],
                                                   scalar=root[:, 0, t:t + 1], in1=mod_tile[:, t, 0:D],
                                                   op0=ALU.mult, op1=ALU.mult)
                ins.then_inc(y_mod_ready, 1)

            def new_x2(c):
                dve.wait_ge(y_ready, 2 * c + 2)
                wait(dve, res_sum_ready, c)
                wait(dve, xs_ready[1], c)
                dve.tensor_tensor(x2[:].rearrange("p t f -> p (t f)"), ps[:, YB, :],
                                  x1[:].rearrange("p t f -> p (t f)"), ALU.add).then_inc(x2_ready, 1)

            def norm_x(n, c):
                inverse_root(c, 1 + n, x_squared, 2 * c + n + 1)
                wait(dve, xsT_ready[n], c)
                for t in range(NT):
                    ins = dve.tensor_scalar(xs_row[n][:, t, :], (x1, x2)[n][:, t, :],
                                            root[:, 1 + n, t:t + 1], None, ALU.mult)
                ins.then_inc(xs_ready[n], 1)

            def gain_in(n, c):
                dve.wait_ge(xsT_ready[n], c + 1)
                wait(dve, xs_gb_ready[n], c)
                dve.tensor_tensor(by_seq(xs_g[n][:]),
                                  ps[:, XTB[n], :].rearrange("p (k b s) -> p k b s", k=KT, s=S),
                                  mod_of(2 * n, c), ALU.mult).then_inc(xs_g_ready[n], 1)

            def ff_input_lo(f):
                dve.wait_ge(ff_hi_ready, f + 1)
                dve.tensor_tensor(ff_lo[:], xs_gb[1][:], ff_hi[:], ALU.subtract).then_inc(ff_lo_ready, 1)

            def hidden(f, j):
                if f is None:
                    return
                n = NJ * f + j
                g, u = ps[:, GU[j % 2], 0:TC], ps[:, GU[j % 2], TC:2 * TC]
                dve.wait_ge(tanh_ready, n + 1)
                wait(dve, h_ready, n)
                dve.scalar_tensor_tensor(out=gate_s[:], in0=gate_t[:, j % 2, :], scalar=1.0, in1=g,
                                         op0=ALU.add, op1=ALU.mult).then_inc(gate_ready, 1)
                dve.wait_ge(gate_ready, n + 1)
                wait(dve, h_lo_ready, NJ * f + max(j - 1, 0))
                dve.scalar_tensor_tensor(out=h_T[:, j % 2, :], in0=gate_s[:], scalar=0.5, in1=u,
                                         op0=ALU.mult, op1=ALU.mult).then_inc(h_ready, 1)

            def result(f):
                if f is None:
                    return
                dve.wait_ge(acc_ready, f + 1)
                dve.wait_ge(res_sum_ready, f + 1)
                wait(dve, res_stored, 16 * f)
                dve.tensor_tensor(res[:].rearrange("p t f -> p (t f)"), ps[:, ACC, :],
                                  res_sum[:].rearrange("p t f -> p (t f)"), ALU.add).then_inc(res_ready, 1)

            def attention(c, l, f):
                shift_scores(c, l, 0)
                hidden(f, 7 * l)
                shift_scores(c, l, 1)
                shift_scores(c, l, 2)
                shift_scores(c, l, 3)
                norm_output(c, l, 0)
                if l == 0:
                    hidden(f, 1)
                norm_output(c, l, 1)
                if l == 0:
                    hidden(f, 2)
                else:
                    result(f)
                output_lo(c, l)

            def turn(c, f):
                if c is not None:
                    input_lo(c, 0)
                if f is not None:
                    gain_in(1, f)
                if c is not None:
                    values(c, 0)
                if f is not None:
                    ff_input_lo(f)
                if c is None:
                    for j in range(NJ):
                        hidden(f, j)
                    result(f)
                    return
                attention(c, 0, f)
                hidden(f, 3)
                modulate_y(c)
                hidden(f, 4)
                hidden(f, 5)
                norm_x(0, c)
                hidden(f, 6)
                gain_in(0, c)
                input_lo(c, 1)
                values(c, 1)
                attention(c, 1, f)
                new_x2(c)
                norm_x(1, c)

            turn(0, None)
            turn(1, 0)
            with dve.Fori(2, NCH) as c:
                turn(c, c - 1)
            turn(None, NCH - 1)

        @block.tensor
        def _(pe):
            pe.wait_ge(consts_landed, 16 * len(CONSTS))
            pe.wait_ge(silu_ready, 1)
            pe.matmul(ps[0:NB, 0, :], condT_silu[:], wcT[:], start=True, stop=True).then_inc(mod_ready, 1)
            for i in range(4 * KT):
                mm = pe.matmul(ps[:, 1, NB * i:NB * i + NB], modw[:, i // KT, P * (i % KT):P * (i % KT) + P],
                               condT[:], start=True, stop=True)
            mm.then_inc(mod_ready, 1)

            def split_product(dst, pairs, first=True, last=True):
                terms = [(x[i], y[j]) for x, y in pairs for i, j in ((0, 0), (0, 1), (1, 0))]
                for n, (x, y) in enumerate(terms):
                    mm = pe.matmul(dst, x, y, start=first and n == 0, stop=last and n == len(terms) - 1,
                                   skip_group_check=True)
                return mm

            def project(c, l):
                w = "k0 q0 v0".split() if l == 0 else "k1 q1 v1".split()
                pe.wait_ge(w_lo_done, WCOL[w[2]] // WBLK + 1)
                pe.wait_ge(in_lo_ready, 2 * c + l + 1)
                xs = [(in_hi[:, k, :], in_lo[:, k, :]) for k in range(KT)]
                for name, b, done in ((w[0], KB, k_ready), (w[1], QB, q_ready)):
                    for m in range(KT):
                        mm = split_product(ps[:, b, TC * m:TC * m + TC],
                                           [(w_parts(name, k, P * m, P), xs[k]) for k in range(KT)],
                                           first=m == 0)
                    mm.then_inc(done, 1)
                if l == 0:
                    wait(pe, x2_ready, c)
                for t in range(NT):
                    rows = slice(P * t, P * t + P)
                    mm = split_product(ps[:, VB, D * t:D * t + D],
                                       [((in_hi[:, k, rows], in_lo[:, k, rows]), w_parts(w[2], k, 0, D))
                                        for k in range(KT)], first=t == 0)
                mm.then_inc(v_ready, 1)

            def scores(c, l, i):
                t, m = divmod(i, KT)
                n = NI * (2 * c + l) + i
                if i == 0:
                    pe.wait_ge(q_copied, 2 * c + l + 1)
                    pe.wait_ge(kdiag_landed, 16 * HH * (2 * c + l + 1))
                wait(pe, shifted_ready, n)
                if l == 0:
                    pe.matmul(ps[:, SC, :], seq_sel[:], mask_neg[:].rearrange("q h s -> q (h s)"),
                              start=True, stop=False, skip_group_check=True)
                for b in range(2):
                    at = S * (2 * t + b)
                    mm = pe.matmul(ps[S * b:S * b + S, SC, :], q_T[:, m, at:at + S],
                                   k_diag[:, m, :, at:at + S], start=l == 1, stop=True,
                                   skip_group_check=True)
                mm.then_inc(scores_ready, 1)

            def transpose_probs(c, l, i):
                n = NI * (2 * c + l) + i
                pe.wait_ge(probs_ready, n + 1)
                wait(pe, pT_copied, n)
                for j in range(4):
                    mm = pe.transpose(ps[:, PT, P * j:P * j + P], probs[:, i % 2, P * j:P * j + P], ident[:])
                mm.then_inc(pT_ready, 1)

            def weigh_values(c, l, i):
                t, m = divmod(i, KT)
                n = NI * (2 * c + l) + i
                if i == 0:
                    pe.wait_ge(v_copied, 2 * c + l + 1)
                pe.wait_ge(pT_copied, n + 1)
                for j in range(4):
                    pair = 4 * m + j
                    for b in range(2):
                        mm = pe.matmul(ps[S * b:S * b + S, OB[t], 2 * DE * pair:2 * DE * (pair + 1)],
                                       probs_T[:, i % 2, P * j + S * b:P * j + S * b + S],
                                       v_pairs[:, t, b, pair, :], start=True, stop=True)
                mm.then_inc(pv_ready, 1)

            def transpose_output(c, l):
                pe.wait_ge(o_ready, NT * (2 * c + l + 1))
                for t in range(NT):
                    for k in range(KT):
                        at = P * (KT * t + k)
                        mm = pe.transpose(ps[:, OTB, at:at + P], o_row[:, t, P * k:P * k + P], ident[:])
                mm.then_inc(oT_ready, 1)

            def output_product(c, l):
                if l == 0:
                    pe.wait_ge(w_lo_done, WCOL["o0"] // WBLK + 1)
                pe.wait_ge(o_lo_ready, 2 * c + l + 1)
                for t in range(NT):
                    mm = split_product(ps[:, YB, D * t:D * t + D],
                                       [((o_hi[:, t, k, :], o_lo[:, t, k, :]),
                                         w_parts("o0" if l == 0 else "o1", k, 0, D)) for k in range(KT)],
                                       first=t == 0)
                mm.then_inc(y_ready, 1)

            def transpose_normed(n, c):
                pe.wait_ge(xs_ready[n], c + 1)
                for k in range(KT):
                    for t in range(NT):
                        at = TC * k + P * t
                        mm = pe.transpose(ps[:, XTB[n], at:at + P], xs_row[n][:, t, P * k:P * k + P], ident[:])
                mm.then_inc(xsT_ready[n], 1)

            def hidden(f, j):
                if f is None:
                    return
                if j == 0:
                    pe.wait_ge(w_lo_done, NWB)
                    pe.wait_ge(ff_lo_ready, f + 1)
                wait(pe, h_ready, NJ * f + max(j - 1, 0))
                for n, name in enumerate(("gate", "hid")):
                    mm = split_product(ps[:, GU[j % 2], TC * n:TC * n + TC],
                                       [(w_parts(name, k, P * j, P, HID), (ff_hi[:, k, :], ff_lo[:, k, :]))
                                        for k in range(KT)], first=n == 0)
                mm.then_inc(gu_ready, 1)
                if j >= 1:
                    hidden_out(f, j - 1)

            def hidden_out(f, j):
                if f is None:
                    return
                if j == 0:
                    wait(pe, res_ready, f)
                pe.wait_ge(h_lo_ready, NJ * f + j + 1)
                for t in range(NT):
                    rows = slice(P * t, P * t + P)
                    mm = split_product(ps[:, ACC, D * t:D * t + D],
                                       [((h_hi[:, j % 2, rows], h_lo[:, j % 2, rows]),
                                         w_parts("out", j, 0, D))],
                                       first=j == 0 and t == 0, last=j == NJ - 1)
                if j == NJ - 1:
                    mm.then_inc(acc_ready, 1)

            def attention(c, l, f):
                scores(c, l, 0)
                hidden(f, 7 * l)
                for i in range(1, NI):
                    scores(c, l, i)
                    transpose_probs(c, l, i - 1)
                    weigh_values(c, l, i - 1)
                if l == 0:
                    hidden(f, 1)
                transpose_probs(c, l, NI - 1)
                weigh_values(c, l, NI - 1)
                if l == 0:
                    hidden(f, 2)
                else:
                    hidden_out(f, NJ - 1)
                transpose_output(c, l)
                if l == 0:
                    hidden(f, 3)
                output_product(c, l)

            def turn(c, f):
                if c is not None:
                    project(c, 0)
                if f is not None:
                    transpose_normed(1, f)
                if c is None:
                    for j in range(NJ):
                        hidden(f, j)
                    hidden_out(f, NJ - 1)
                    return
                attention(c, 0, f)
                hidden(f, 4)
                hidden(f, 5)
                hidden(f, 6)
                transpose_normed(0, c)
                project(c, 1)
                attention(c, 1, f)

            pe.wait_ge(modT_done, 1)
            pe.wait_ge(mod_chain, 3)
            pe.wait_ge(mask_ready, 1)
            pe.wait_ge(sel_ready, 1)
            turn(0, None)
            turn(1, 0)
            with pe.Fori(2, NCH) as c:
                turn(c, c - 1)
            turn(None, NCH - 1)


def kernel(**inputs):
    import numpy as np
    import concourse.bacc as bacc
    from concourse.bass_utils import run_bass_kernel_spmd

    def T(name):
        return np.asarray(inputs[name]).T

    def tiles(w):
        return w.reshape(-1, P, w.shape[1]).transpose(1, 0, 2).reshape(P, -1)

    def cols(name):
        return np.asarray(inputs[name]).reshape(KT, P).T

    names = ["L0_cond_Wk", "L0_cond_Wq", "L0_cond_Wv", "L0_cond_Wo", "L1_cond_Wk", "L1_cond_Wq",
             "L1_cond_Wv", "L1_cond_Wo", "L1_cond_gate_w", "L1_cond_hid_w", "L1_cond_out_w"]
    x = np.asarray(inputs["x"]).reshape(NCH, NT, P, D)
    arrays = {
        "x": x,
        "xT": x.reshape(NCH, TC, KT, P).transpose(0, 3, 2, 1),
        "weights": np.concatenate([tiles(T(n)) for n in names], axis=1),
        "condT": T("cond_256"),
        "wcT": T("L0_cond_Wc"),
        "bc": np.asarray(inputs["L0_cond_bc"]),
        "rms": np.asarray(inputs["L0_cond_rms_scale"]),
        "g1wT": T("L1_cond_g1w"), "b1wT": T("L1_cond_b1w"),
        "g2wT": T("L1_cond_g2w"), "b2wT": T("L1_cond_b2w"),
        "modb": np.concatenate([cols("L1_cond_" + n) for n in ("g1b", "b1b", "g2b", "b2b")], axis=1),
        "mask": np.asarray(inputs["mask_SxS_bk1"]),
    }
    arrays = {n: np.ascontiguousarray(v) for n, v in arrays.items()}

    nc = bacc.Bacc("TRN2", target_bir_lowering=False, num_devices=1)
    aps = {n: nc.dram_tensor(f"in_{n}", v.shape, mybir.dt.from_np(v.dtype), kind="ExternalInput").ap()
           for n, v in arrays.items()}
    out = nc.dram_tensor("out", (NCH, NT, P, D), F32, kind="ExternalOutput").ap()
    build(nc, aps, out)
    r = run_bass_kernel_spmd(nc, [{f"in_{n}": v for n, v in arrays.items()}], core_ids=[0])
    return r.results[0]["out"].reshape(NB, S, D)
```

```python
from contextlib import ExitStack

import concourse.bass as bass
from concourse import mybir

ALU = mybir.AluOpType
ACT = mybir.ActivationFunctionType
AXX = mybir.AxisListType.X
F32 = mybir.dt.float32
F32R = mybir.dt.float32r
I32 = mybir.dt.int32
U8 = mybir.dt.uint8
BF16 = mybir.dt.bfloat16

P = 128
NB, S, D = 32, 64, 256
H, DH = 16, 16
DT = 64
HID = 1024
KT = D // P
HH = H // KT
NP = H // 2
DE = DH + 1
NT = 2
TC = NT * P
NCH = NB * S // TC
CB = TC // S
NI = NT * KT
NJ = HID // P
EPS = 1e-6
SCALE = DH ** -0.5
BIG = 1e30
NEWTON = 3
CHAIN = 3 + 3 * NEWTON
ROOT_SEED = 0x5F3759DF

WCOL = {w: 512 * n for n, w in enumerate(["k0", "q0", "v0", "o0", "k1", "q1", "v1", "o1"])}
WCOL["gate"], WCOL["hid"], WCOL["out"] = 4096, 4096 + 2 * HID, 4096 + 4 * HID
WBLK = 512
NWB = (4096 + 6 * HID) // WBLK
NSTAGE = 3

L0, L1, FF = 0, 1, 2
NOW, BEFORE = 0, -1

GU_BANK = [1, 0, 2, 0, 2, 0, 2, 0]
ACC_BANK = 1
KEYS_BANK = [7, 7]
QUERIES_BANK = [5, 4]
VALUES_BANK = [3, 3]
SCORES_BANK = [[6, 5, 7, 6], [5, 7, 6, 7]]
PROBS_T_BANK = [[3, 4, 7, 4], [5, 4, 6, 7]]
OUT_BANK = [[3, 5], [5, 7]]
OUT_T_BANK = [4, 7]
Y_BANK = [3, 5]
XS_T_BANK = [6, 2]


def idle(T, lag):
    return isinstance(T, int) and not 0 <= T - lag < NCH


def first(T, lag):
    return isinstance(T, int) and T == lag


def done(T, lag, per, nth, turn=NOW):
    count = per * (T + turn - lag) + nth
    return min(count, per * NCH) if isinstance(T, int) else count


def wait(eng, s, count):
    if not (isinstance(count, int) and count <= 0):
        eng.wait_ge(s, count)


def weight_blocks(T, slot):
    if first(T, L0):
        return [3 + slot] if slot < 5 else []
    return [8 + slot] if first(T, L1) else []


def load_blocks(T, slot):
    return [n + NSTAGE for n in weight_blocks(T, slot) if n + NSTAGE < NWB]


def build(nc, a, out):
    ctx = ExitStack()
    with ctx:
        def sb(name, shape, dt=F32):
            return ctx.enter_context(nc.sbuf_tensor(name, shape, dt))

        def sem(name):
            return ctx.enter_context(nc.semaphore(name))

        ps = ctx.enter_context(nc.psum_tensor("ps", [P, 8, 512], F32))
        mod_dram = nc.dram_tensor("mod_rows_dram", [NB, 2 * D], F32, kind="Internal").ap()

        w_stage = sb("w_stage", [P, NSTAGE, WBLK])
        w_hi = sb("w_hi", [P, NWB * WBLK], F32R)
        w_lo = sb("w_lo", [P, NWB * WBLK], F32R)
        ident = sb("ident", [P, P])
        seq_sel = sb("seq_sel", [S, P], F32R)
        mask_u8 = sb("mask_u8", [S, S], U8)
        mask_neg = sb("mask_neg", [S, HH, S], F32R)
        condT = sb("condT", [DT, NB])
        condT_silu = sb("condT_silu", [DT, NB])
        modb = sb("modb", [P, 4 * KT])
        modT = sb("modT", [P, 4, KT, NB])

        x_T = sb("x_T", [P, KT, TC])
        x_row = sb("x_row", [P, NT, D])
        in_hi = [sb(f"in_hi{l}", [P, KT, TC], F32R) for l in range(2)]
        in_lo = [sb(f"in_lo{l}", [P, KT, TC], F32R) for l in range(2)]
        ff_hi = sb("ff_hi", [P, KT, TC], F32R)
        ff_lo = sb("ff_lo", [P, KT, TC], F32R)
        q_T = [sb(f"q_T{l}", [P, KT, TC]) for l in range(2)]
        k_T = [sb(f"k_T{l}", [P, KT, TC]) for l in range(2)]
        k_diag = [sb(f"k_diag{l}", [P, KT, HH, TC]) for l in range(2)]
        v_pairs = [sb(f"v_pairs{l}", [P, NT, 2, NP, 2 * DE]) for l in range(2)]
        row_max = [sb(f"row_max{l}", [P, HH]) for l in range(2)]
        shifted = sb("shifted", [P, 2, HH * S])
        probs = sb("probs", [P, 2, HH * S])
        probs_T = sb("probs_T", [P, 2, 4 * P])
        inv_sum = [sb(f"inv_sum{l}", [P, H]) for l in range(2)]
        o_row = sb("o_row", [P, NT, D])
        o_hi = sb("o_hi", [P, NT, KT, P], F32R)
        o_lo = sb("o_lo", [P, NT, KT, P], F32R)
        mod_tile = sb("mod_tile", [P, NT, 2 * D])
        y_mod = sb("y_mod", [P, NT, D])
        x1 = sb("x1", [P, NT, D])
        x1_kept = sb("x1_kept", [P, NT, D])
        x2 = sb("x2", [P, NT, D])
        sq_junk = sb("sq_junk", [P, 3, NT, D], BF16)
        sumsq = sb("sumsq", [P, 3, NT])
        mean_sq = sb("mean_sq", [P, 3, NT])
        root_bits = sb("root_bits", [P, 3, NT], I32)
        root = sb("root", [P, 3, NT])
        root_i = sb("root_i", [P, 3, NT], I32)
        root_a = sb("root_a", [P, 3, NT])
        root_b = sb("root_b", [P, 3, NT])
        xs_row = [sb(f"xs_row{n}", [P, NT, D]) for n in range(2)]
        xs_g = [sb(f"xs_g{n}", [P, KT, TC]) for n in range(2)]
        gate_t = w_stage[:, 0, :].rearrange("p (j s) -> p j s", j=2)
        h_T = w_stage[:, 1, :].rearrange("p (j s) -> p j s", j=2)
        gate_s = w_stage[:, 2, 0:TC]
        h_hi = sb("h_hi", [P, 2, TC], F32R)
        h_lo = sb("h_lo", [P, 2, TC], F32R)
        sum_next = sb("sum_next", [P, NT, D])
        res_sum = sb("res_sum", [P, NT, D])
        res = sb("res", [P, NT, D])
        wcT = x2[0:DT].rearrange("p t f -> p (t f)")
        bc_rows = sum_next[0:NB].rearrange("p t f -> p (t f)")
        mod_rows = res_sum[0:NB].rearrange("p t f -> p (t f)")
        rms_rows = res[0:NB, 0, :]
        modw = [t[0:DT, k, :] for t in xs_g for k in range(KT)]

        w_landed = [sem(f"w_landed{n}") for n in range(NSTAGE)]
        w_hi_done, w_lo_done = sem("w_hi_done"), sem("w_lo_done")
        consts_landed, pool_set = sem("consts_landed"), sem("pool_set")
        ident_ready, v_ones_set = sem("ident_ready"), sem("v_ones_set")
        sel_ready, mask_ready = sem("sel_ready"), sem("mask_ready")
        silu_ready, mod_ready = sem("silu_ready"), sem("mod_ready")
        mod_chain, modT_done, mod_stored = sem("mod_chain"), sem("modT_done"), sem("mod_stored")
        xT_landed, xrow_landed, modtile_landed = sem("xT_landed"), sem("xrow_landed"), sem("modtile_landed")
        res_stored = sem("res_stored")
        def by_layer(name):
            return [sem(f"{name}{l}") for l in range(2)]

        in_hi_ready, in_lo_ready = by_layer("in_hi_ready"), by_layer("in_lo_ready")
        k_ready, q_ready, v_ready = by_layer("k_ready"), by_layer("q_ready"), by_layer("v_ready")
        k_copied, q_copied, v_copied = by_layer("k_copied"), by_layer("q_copied"), by_layer("v_copied")
        kdiag_landed = by_layer("kdiag_landed")
        scores_ready, max_ready, max_clamped = by_layer("scores_ready"), by_layer("max_ready"), sem("max_clamped")
        shifted_ready, probs_ready = by_layer("shifted_ready"), by_layer("probs_ready")
        pT_ready, pT_copied = by_layer("pT_ready"), by_layer("pT_copied")
        pv_ready, inv_ready, o_ready = by_layer("pv_ready"), by_layer("inv_ready"), by_layer("o_ready")
        oT_ready, o_hi_ready, o_lo_ready = by_layer("oT_ready"), by_layer("o_hi_ready"), by_layer("o_lo_ready")
        y_ready = by_layer("y_ready")
        squared = [sem(f"squared{r}") for r in range(3)]
        newton = [sem(f"newton{r}") for r in range(3)]
        shift_ready, y_mod_ready = sem("shift_ready"), sem("y_mod_ready")
        x1_ready, x1_kept_ready, x2_ready = sem("x1_ready"), sem("x1_kept_ready"), sem("x2_ready")
        sum_ready, sum_moved = sem("sum_ready"), sem("sum_moved")
        xs_ready, xsT_ready = by_layer("xs_ready"), by_layer("xsT_ready")
        xs_g_ready, xs_gb_ready = by_layer("xs_g_ready"), by_layer("xs_gb_ready")
        ff_hi_ready, ff_lo_ready = sem("ff_hi_ready"), sem("ff_lo_ready")
        gu_ready, tanh_ready, gate_ready = sem("gu_ready"), sem("tanh_ready"), sem("gate_ready")
        h_ready, h_hi_ready, h_lo_ready = sem("h_ready"), sem("h_hi_ready"), sem("h_lo_ready")
        h_used, res_ready = sem("h_used"), sem("res_ready")

        block = ctx.enter_context(nc.Block())

        CONSTS = (
            (condT[:], a["condT"]), (wcT[:], a["wcT"]), (mask_u8[:], a["mask"]),
            (bc_rows[:], a["bc"].partition_broadcast(NB)),
            (rms_rows[:], a["rms"].partition_broadcast(NB)),
            (modw[0], a["g1wT"]), (modw[1], a["b1wT"]),
            (modw[2], a["g2wT"]), (modw[3], a["b2wT"]),
            (modb[:], a["modb"]),
        )

        def by_seq(t):
            return t.rearrange("p k (b s) -> p k b s", s=S)

        def mod_of(which, c):
            return modT[:, which, :, bass.ds(c * CB, CB)].unsqueeze(3).to_broadcast([P, KT, CB, S])

        def w_parts(name, k, c0, n, width=D):
            at = WCOL[name] + k * width + c0
            return w_hi[:, at:at + n], w_lo[:, at:at + n]

        @block.sync
        def _(sp):
            def load_w(n):
                wait(sp, w_hi_done, n - NSTAGE + 1)
                wait(sp, w_lo_done, n - NSTAGE + 1)
                sp.dma_start(w_stage[:, n % NSTAGE, :], a["weights"][:, n * WBLK:(n + 1) * WBLK])\
                    .then_inc(w_landed[n % NSTAGE], 16)

            def load_more(T, slot):
                for n in load_blocks(T, slot):
                    load_w(n)

            def load_tokens(T):
                wait(sp, in_lo_ready[0], T)
                sp.dma_start(x_T[:], a["xT"][bass.ds(T, 1)].rearrange("a p k s -> (a p) k s"))\
                    .then_inc(xT_landed, 16)

            def tokens(T):
                if not (idle(T, L0) or first(T, L0)):
                    load_tokens(T)

            def rows(T):
                if idle(T, L0):
                    return
                if first(T, L0):
                    sp.wait_ge(mod_stored, 16)
                wait(sp, x1_ready, T)
                sp.dma_start(x_row[:], a["x"][bass.ds(T, 1)].rearrange("a t p f -> (a p) t f"))\
                    .then_inc(xrow_landed, 16)
                wait(sp, y_mod_ready, T)
                for b in range(CB):
                    sp.dma_start(mod_tile[S * (b % 2):S * (b % 2) + S, b // 2, :],
                                 mod_dram[bass.ds(T * CB + b, 1)].rearrange("a n -> (a n)")
                                 .partition_broadcast(S)).then_inc(modtile_landed, 16)

            def keys(T, l):
                if idle(T, l):
                    return
                if first(T, l):
                    sp.wait_ge(pool_set, 2 + 2 * l)
                sp.wait_ge(k_copied[l], T - l + 1)
                for h in range(HH):
                    own = slice(DH * h, DH * h + DH)
                    sp.dma_start(k_diag[l][own, :, h, :], k_T[l][own, :, :]).then_inc(kdiag_landed[l], 16)

            def turn(T):
                tokens(T)
                keys(T, 0)
                keys(T, 1)
                load_more(T, 0)
                rows(T)
                load_more(T, 1)
                load_more(T, 2)
                load_more(T, 3)
                load_more(T, 4)
                load_more(T, 5)
                load_more(T, 6)
                load_more(T, 7)
                load_more(T, 8)
                load_more(T, 9)
                load_more(T, 10)
                load_more(T, 11)

            load_tokens(0)
            for n in range(NSTAGE):
                load_w(n)
            for dst, src in CONSTS:
                sp.dma_start(dst, src).then_inc(consts_landed, 16)
            for n in range(NSTAGE, 2 * NSTAGE):
                load_w(n)
            turn(0)
            turn(1)
            turn(2)
            with sp.Fori(3, NCH) as T:
                turn(T)
            turn(NCH)

        @block.gpsimd
        def _(pool):
            pool.memset(ident[:], 0.0).then_inc(pool_set, 1)
            pool.wait_ge(pool_set, 1)
            pool.affine_select(out=ident[:], in_=ident[:], compare_op=ALU.not_equal, fill=1.0,
                               base=0, pattern=[[-1, P]], channel_multiplier=1).then_inc(ident_ready, 1)
            for l in range(2):
                pool.memset(k_diag[l][:], 0.0).then_inc(pool_set, 1)
                pool.memset(v_pairs[l][:], 0.0).then_inc(pool_set, 1)
                pool.wait_ge(pool_set, 2 * l + 3)
                pool.memset(v_pairs[l][0:S, :, :, :, DH:DE], 1.0).then_inc(v_ones_set, 1)
                pool.wait_ge(v_ones_set, 2 * l + 1)
                pool.memset(v_pairs[l][S:P, :, :, :, DE + DH:2 * DE], 1.0).then_inc(v_ones_set, 1)
                pool.wait_ge(v_ones_set, 2 * l + 2)
                if l == 0:
                    pool.wait_ge(mod_chain, 3)
                    pool.dma_start(mod_dram, mod_rows[:]).then_inc(mod_stored, 16)

            def shift_in(T):
                if idle(T, L0):
                    return
                pool.wait_ge(xrow_landed, 16 * (T + 1))
                pool.wait_ge(modtile_landed, 16 * CB * (T + 1))
                pool.tensor_tensor(x_row[:], x_row[:], mod_tile[:, :, D:2 * D], ALU.add)\
                    .then_inc(shift_ready, 1)

            def new_x1(T):
                if idle(T, L0):
                    return
                pool.wait_ge(y_mod_ready, T + 1)
                pool.wait_ge(shift_ready, T + 1)
                wait(pool, x1_kept_ready, T)
                wait(pool, xs_ready[0], T)
                pool.tensor_tensor(x1[:], y_mod[:], x_row[:], ALU.add).then_inc(x1_ready, 1)

            def bias_in(T, n):
                lag = (L0, FF)[n]
                if idle(T, lag):
                    return
                pool.wait_ge(xs_g_ready[n], T - lag + 1)
                pool.tensor_tensor(by_seq(xs_g[n][:]), by_seq(xs_g[n][:]), mod_of(2 * n + 1, T - lag),
                                   ALU.add).then_inc(xs_gb_ready[n], 1)

            def sum_residuals(T):
                if idle(T, L1):
                    return
                pool.wait_ge(x2_ready, T)
                wait(pool, sum_moved, T - 1)
                pool.tensor_tensor(sum_next[:], x1_kept[:], x2[:], ALU.add).then_inc(sum_ready, 1)

            def store(T):
                if idle(T, FF):
                    return
                pool.wait_ge(res_ready, T - 1)
                pool.dma_start(out[bass.ds(T - 2, 1)].rearrange("a t p f -> (a p) t f"), res[:])\
                    .then_inc(res_stored, 16)

            def hidden_lo(T, j):
                if idle(T, FF):
                    return
                pool.wait_ge(h_hi_ready, NJ * (T - 2) + j + 1)
                pool.tensor_tensor(h_lo[:, j % 2, :], h_T[:, j % 2, :], h_hi[:, j % 2, :],
                                   ALU.subtract).then_inc(h_lo_ready, 1)

            def turn(T):
                bias_in(T, 1)
                hidden_lo(T, 0)
                hidden_lo(T, 1)
                hidden_lo(T, 2)
                shift_in(T)
                hidden_lo(T, 3)
                new_x1(T)
                hidden_lo(T, 4)
                hidden_lo(T, 5)
                bias_in(T, 0)
                hidden_lo(T, 6)
                hidden_lo(T, 7)
                sum_residuals(T)
                store(T)

            pool.wait_ge(modT_done, 1)
            turn(0)
            turn(1)
            turn(2)
            with pool.Fori(3, NCH) as T:
                turn(T)
            turn(NCH)
            turn(NCH + 1)
            pool.wait_ge(res_stored, 16 * NCH)

        @block.scalar
        def _(act):
            def weights_hi(*ns):
                for n in ns:
                    act.wait_ge(w_landed[n % NSTAGE], 16 * (n // NSTAGE + 1))
                    act.activation(w_hi[:, n * WBLK:(n + 1) * WBLK], w_stage[:, n % NSTAGE, :], ACT.Copy)\
                        .then_inc(w_hi_done, 1)

            def more_weights(T, slot):
                weights_hi(*weight_blocks(T, slot))

            def input_hi(T, l):
                if idle(T, L0):
                    return
                if l == 0:
                    act.wait_ge(xT_landed, 16 * (T + 1))
                    wait(act, v_ready[0], T)
                else:
                    act.wait_ge(xs_gb_ready[0], T + 1)
                    wait(act, v_ready[1], T)
                act.activation(in_hi[l][:], (x_T if l == 0 else xs_g[0])[:], ACT.Copy)\
                    .then_inc(in_hi_ready[l], 1)

            def condition(T):
                if first(T, L0):
                    act.wait_ge(consts_landed, 16 * len(CONSTS))
                    act.activation(condT_silu[:], condT[:], ACT.Silu).then_inc(silu_ready, 1)

            def ff_input_hi(T):
                if idle(T, FF):
                    return
                act.wait_ge(xs_gb_ready[1], T - 1)
                wait(act, gu_ready, NJ * (T - 2))
                act.activation(ff_hi[:], xs_g[1][:], ACT.Copy).then_inc(ff_hi_ready, 1)

            def copy_keys(T, l):
                if idle(T, l):
                    return
                act.wait_ge(k_ready[l], T - l + 1)
                wait(act, kdiag_landed[l], 16 * HH * (T - l))
                act.activation(k_T[l][:], ps[:, KEYS_BANK[l], :], ACT.Copy).then_inc(k_copied[l], 1)

            def copy_queries(T, l):
                if idle(T, l):
                    return
                act.wait_ge(q_ready[l], T - l + 1)
                act.activation(q_T[l][:], ps[:, QUERIES_BANK[l], :], ACT.Copy).then_inc(q_copied[l], 1)

            def exponentials(T, l, i):
                if idle(T, l):
                    return
                act.wait_ge(shifted_ready[l], NI * (T - l) + i + 1)
                if i >= 2:
                    act.wait_ge(pT_ready[l], NI * (T - l) + i - 1)
                elif l == 0:
                    wait(act, pT_ready[1], done(T, L1, NI, i + 3, BEFORE))
                else:
                    wait(act, pT_ready[0], done(T, L0, NI, i + 3))
                if isinstance(T, int) and i < 2:
                    wait(act, pT_ready[l], done(T, l, NI, i + 3, BEFORE))
                act.activation(probs[:, i % 2, :], shifted[:, i % 2, :], ACT.Exp, scale=SCALE)\
                    .then_inc(probs_ready[l], 1)

            def copy_pT(T, l, i):
                if idle(T, l):
                    return
                act.wait_ge(pT_ready[l], NI * (T - l) + i + 1)
                if i >= 2:
                    act.wait_ge(pv_ready[l], NI * (T - l) + i - 1)
                elif l == 0:
                    wait(act, pv_ready[1], done(T, L1, NI, i + 3, BEFORE))
                else:
                    wait(act, pv_ready[0], done(T, L0, NI, i + 3))
                if isinstance(T, int) and i < 2:
                    wait(act, pv_ready[l], done(T, l, NI, i + 3, BEFORE))
                act.activation(probs_T[:, i % 2, :], ps[:, PROBS_T_BANK[l][i], :], ACT.Copy)\
                    .then_inc(pT_copied[l], 1)

            def output_hi(T, l):
                if idle(T, l):
                    return
                act.wait_ge(oT_ready[l], T - l + 1)
                wait(act, y_ready[1 - l], done(T, 1 - l, 1, 1, BEFORE if l == 0 else NOW))
                if isinstance(T, int):
                    wait(act, y_ready[l], T - l)
                act.activation(o_hi[:], ps[:, OUT_T_BANK[l], :], ACT.Copy).then_inc(o_hi_ready[l], 1)

            def squares(r, src):
                for t in range(NT):
                    ins = act.activation(sq_junk[:, r, t, :], src(t), ACT.Square,
                                         accum_out=sumsq[:, r, t:t + 1])
                ins.then_inc(squared[r], 1)

            def squares_y(T):
                if idle(T, L0):
                    return
                act.wait_ge(y_ready[0], T + 1)
                wait(act, y_mod_ready, T)
                squares(0, lambda t: ps[:, Y_BANK[0], D * t:D * t + D])

            def squares_x(T, n):
                if idle(T, n):
                    return
                act.wait_ge((x1_ready, x2_ready)[n], T - n + 1)
                wait(act, xs_ready[n], T - n)
                squares(1 + n, lambda t: (x1, x2)[n][:, t, :])

            def keep_x1(T):
                if idle(T, L1):
                    return
                act.wait_ge(x1_ready, T)
                wait(act, sum_ready, T - 1)
                act.activation(x1_kept[:], x1[:], ACT.Copy).then_inc(x1_kept_ready, 1)

            def tanh(T, j):
                if idle(T, FF):
                    return
                act.wait_ge(gu_ready, NJ * (T - 2) + j + 1)
                wait(act, gate_ready, NJ * (T - 2) + max(j - 1, 0))
                act.activation(gate_t[:, j % 2, :], ps[:, GU_BANK[j], 0:TC], ACT.Tanh, scale=0.5)\
                    .then_inc(tanh_ready, 1)

            def hidden_hi(T, j):
                if idle(T, FF):
                    return
                act.wait_ge(h_ready, NJ * (T - 2) + j + 1)
                wait(act, h_used, NJ * (T - 2) + j - 1)
                act.activation(h_hi[:, j % 2, :], h_T[:, j % 2, :], ACT.Copy).then_inc(h_hi_ready, 1)

            def turn(T):
                keep_x1(T)
                input_hi(T, 0)
                condition(T)
                copy_keys(T, 1)
                copy_keys(T, 0)
                ff_input_hi(T)
                more_weights(T, 0)
                tanh(T, 0)
                copy_queries(T, 1)
                hidden_hi(T, 0)
                more_weights(T, 1)
                copy_queries(T, 0)
                tanh(T, 1)
                tanh(T, 2)
                exponentials(T, 0, 0)
                hidden_hi(T, 1)
                more_weights(T, 2)
                exponentials(T, 0, 1)
                copy_pT(T, 0, 0)
                exponentials(T, 0, 2)
                copy_pT(T, 0, 1)
                exponentials(T, 0, 3)
                copy_pT(T, 0, 2)
                copy_pT(T, 0, 3)
                more_weights(T, 3)
                exponentials(T, 1, 0)
                more_weights(T, 4)
                hidden_hi(T, 2)
                output_hi(T, 0)
                tanh(T, 3)
                exponentials(T, 1, 1)
                tanh(T, 4)
                copy_pT(T, 1, 0)
                squares_y(T)
                copy_pT(T, 1, 1)
                exponentials(T, 1, 2)
                exponentials(T, 1, 3)
                more_weights(T, 5)
                copy_pT(T, 1, 2)
                hidden_hi(T, 3)
                copy_pT(T, 1, 3)
                more_weights(T, 6)
                tanh(T, 5)
                squares_x(T, 0)
                hidden_hi(T, 4)
                output_hi(T, 1)
                tanh(T, 6)
                more_weights(T, 7)
                more_weights(T, 8)
                hidden_hi(T, 5)
                tanh(T, 7)
                more_weights(T, 9)
                input_hi(T, 1)
                hidden_hi(T, 6)
                squares_x(T, 1)
                more_weights(T, 10)
                hidden_hi(T, 7)
                more_weights(T, 11)

            weights_hi(0, 1, 2)
            turn(0)
            turn(1)
            turn(2)
            with act.Fori(3, NCH) as T:
                turn(T)
            turn(NCH)
            turn(NCH + 1)

        @block.vector
        def _(dve):
            def set_up_mask(T):
                if not first(T, L0):
                    return
                dve.wait_ge(consts_landed, 16 * len(CONSTS))
                dve.tensor_scalar(mask_neg[:], mask_u8[:].unsqueeze(1).to_broadcast([S, HH, S]), -BIG,
                                  None, ALU.mult).then_inc(mask_ready, 1)
                dve.wait_ge(ident_ready, 1)
                dve.tensor_copy(seq_sel[:].rearrange("q (a r) -> q a r", a=2),
                                ident[0:S, 0:S].unsqueeze(1).to_broadcast([S, 2, S])).then_inc(sel_ready, 1)

            def set_up_modulations(T):
                if not first(T, L0):
                    return
                dve.wait_ge(mod_ready, 1)
                dve.tensor_tensor(mod_rows[:, D:2 * D], ps[0:NB, 0, 0:D], bc_rows[:, 0:D], ALU.add)\
                    .then_inc(mod_chain, 1)
                dve.tensor_tensor(mod_rows[:, 0:D], ps[0:NB, 0, D:2 * D], bc_rows[:, D:2 * D], ALU.add)\
                    .then_inc(mod_chain, 1)
                dve.wait_ge(mod_chain, 2)
                dve.scalar_tensor_tensor(out=mod_rows[:, 0:D], in0=mod_rows[:, 0:D], scalar=1.0,
                                         in1=rms_rows[:], op0=ALU.add, op1=ALU.mult).then_inc(mod_chain, 1)
                dve.wait_ge(mod_ready, 2)
                dve.tensor_tensor(modT[:].rearrange("p w k b -> p (w k) b"),
                                  ps[:, 1, 0:4 * KT * NB].rearrange("p (i b) -> p i b", b=NB),
                                  modb[:].unsqueeze(2).to_broadcast([P, 4 * KT, NB]), ALU.add)\
                    .then_inc(modT_done, 1)

            def weights_lo(*ns):
                for n in ns:
                    dve.wait_ge(w_hi_done, n + 1)
                    dve.tensor_tensor(w_lo[:, n * WBLK:(n + 1) * WBLK], w_stage[:, n % NSTAGE, :],
                                      w_hi[:, n * WBLK:(n + 1) * WBLK], ALU.subtract).then_inc(w_lo_done, 1)

            def more_weights(T, slot):
                weights_lo(*weight_blocks(T, slot))

            def input_lo(T, l):
                if idle(T, L0):
                    return
                dve.wait_ge(in_hi_ready[l], T + 1)
                dve.tensor_tensor(in_lo[l][:], (x_T if l == 0 else xs_g[0])[:], in_hi[l][:], ALU.subtract)\
                    .then_inc(in_lo_ready[l], 1)

            def values(T, l):
                if idle(T, l):
                    return
                if first(T, l):
                    dve.wait_ge(v_ones_set, 2 * l + 2)
                dve.wait_ge(v_ready[l], T - l + 1)
                for par in range(2):
                    for b in range(2):
                        ins = dve.tensor_copy(
                            v_pairs[l][S * par:S * par + S, :, b, :, DE * par:DE * par + DH],
                            ps[S * b:S * b + S, VALUES_BANK[l], :].rearrange(
                                "p (t j e d) -> p t j e d", t=NT, j=NP, e=2)[:, :, :, par, :])
                ins.then_inc(v_copied[l], 1)

            def shift_scores(T, l, i):
                if idle(T, l):
                    return
                n = NI * (T - l) + i
                scores = ps[:, SCORES_BANK[l][i], :].rearrange("p (h s) -> p h s", s=S)
                dve.wait_ge(scores_ready[l], n + 1)
                wait(dve, shifted_ready[l], n)
                dve.tensor_reduce(row_max[l][:], scores, AXX, ALU.max).then_inc(max_ready[l], 1)
                dve.wait_ge(max_ready[l], n + 1)
                if l == 0:
                    dve.tensor_scalar(row_max[l][:], row_max[l][:], -BIG / 2, None, ALU.max)\
                        .then_inc(max_clamped, 1)
                    dve.wait_ge(max_clamped, n + 1)
                if i >= 2:
                    dve.wait_ge(probs_ready[l], n - 1)
                elif l == 0:
                    wait(dve, probs_ready[1], done(T, L1, NI, i + 3, BEFORE))
                else:
                    wait(dve, probs_ready[0], done(T, L0, NI, i + 3))
                if isinstance(T, int) and i < 2:
                    wait(dve, probs_ready[l], done(T, l, NI, i + 3, BEFORE))
                dve.tensor_tensor(shifted[:, i % 2, :].rearrange("p (h s) -> p h s", s=S), scores,
                                  row_max[l][:].unsqueeze(2).to_broadcast([P, HH, S]), ALU.subtract)\
                    .then_inc(shifted_ready[l], 1)

            def norm_output(T, l, t):
                if idle(T, l):
                    return
                n = NT * (T - l) + t
                sums = ps[:, OUT_BANK[l][t], 0:H * DE].rearrange("p (h e) -> p h e", e=DE)
                dve.wait_ge(pv_ready[l], NI * (T - l) + KT * t + KT)
                wait(dve, o_ready[l], n)
                if t == 0:
                    wait(dve, oT_ready[1 - l], done(T, 1 - l, 1, 1, BEFORE if l == 0 else NOW))
                    if isinstance(T, int):
                        wait(dve, oT_ready[l], T - l)
                dve.reciprocal(inv_sum[l][:], sums[:, :, DH]).then_inc(inv_ready[l], 1)
                dve.wait_ge(inv_ready[l], n + 1)
                dve.tensor_tensor(o_row[:, t, :].rearrange("p (h d) -> p h d", d=DH), sums[:, :, 0:DH],
                                  inv_sum[l][:].unsqueeze(2).to_broadcast([P, H, DH]), ALU.mult)\
                    .then_inc(o_ready[l], 1)

            def output_lo(T, l):
                if idle(T, l):
                    return
                dve.wait_ge(o_hi_ready[l], T - l + 1)
                dve.tensor_tensor(o_lo[:].rearrange("p t k s -> p (t k s)"), ps[:, OUT_T_BANK[l], :],
                                  o_hi[:].rearrange("p t k s -> p (t k s)"), ALU.subtract)\
                    .then_inc(o_lo_ready[l], 1)

            def inverse_root(c, r):
                at = [CHAIN * c]

                def link(ins):
                    at[0] = at[0] + 1
                    ins.then_inc(newton[r], 1)
                    dve.wait_ge(newton[r], at[0])

                m, bits, guess, y = mean_sq[:, r, :], root_bits[:, r, :], root_i[:, r, :], root[:, r, :]
                dve.wait_ge(squared[r], c + 1)
                link(dve.tensor_scalar(m, sumsq[:, r, :], 1.0 / D, EPS, ALU.mult, ALU.add))
                link(dve.tensor_scalar(bits, m.bitcast(I32), 1, None, ALU.logical_shift_right))
                link(dve.tensor_scalar(guess, bits, -1, ROOT_SEED, ALU.mult, ALU.add))
                for k in range(NEWTON):
                    y0 = guess.bitcast(F32) if k == 0 else y
                    link(dve.tensor_tensor(root_a[:, r, :], y0, y0, ALU.mult))
                    link(dve.scalar_tensor_tensor(out=root_b[:, r, :], in0=root_a[:, r, :], scalar=-0.5,
                                                  in1=m, op0=ALU.mult, op1=ALU.mult))
                    link(dve.scalar_tensor_tensor(out=y, in0=root_b[:, r, :], scalar=1.5, in1=y0,
                                                  op0=ALU.add, op1=ALU.mult))

            def modulate_y(T):
                if idle(T, L0):
                    return
                wait(dve, y_mod_ready, T)
                inverse_root(T, 0)
                dve.wait_ge(modtile_landed, 16 * CB * (T + 1))
                wait(dve, x1_ready, T)
                for t in range(NT):
                    ins = dve.scalar_tensor_tensor(
                        out=y_mod[:, t, :], in0=ps[:, Y_BANK[0], D * t:D * t + D],
                        scalar=root[:, 0, t:t + 1], in1=mod_tile[:, t, 0:D], op0=ALU.mult, op1=ALU.mult)
                ins.then_inc(y_mod_ready, 1)

            def new_x2(T):
                if idle(T, L1):
                    return
                dve.wait_ge(y_ready[1], T)
                dve.wait_ge(x1_kept_ready, T)
                wait(dve, sum_ready, T - 1)
                wait(dve, xs_ready[1], T - 1)
                dve.tensor_tensor(x2[:].rearrange("p t f -> p (t f)"), ps[:, Y_BANK[1], :],
                                  x1_kept[:].rearrange("p t f -> p (t f)"), ALU.add).then_inc(x2_ready, 1)

            def norm_x(T, n):
                if idle(T, n):
                    return
                wait(dve, xs_ready[n], T - n)
                inverse_root(T - n, 1 + n)
                wait(dve, xsT_ready[n], T - n)
                for t in range(NT):
                    ins = dve.tensor_scalar(xs_row[n][:, t, :], (x1, x2)[n][:, t, :],
                                            root[:, 1 + n, t:t + 1], None, ALU.mult)
                ins.then_inc(xs_ready[n], 1)

            def gain_in(T, n):
                c = T - (L0, FF)[n]
                if idle(T, (L0, FF)[n]):
                    return
                dve.wait_ge(xsT_ready[n], c + 1)
                wait(dve, (in_lo_ready[1], ff_lo_ready)[n], c)
                dve.tensor_tensor(by_seq(xs_g[n][:]),
                                  ps[:, XS_T_BANK[n], :].rearrange("p (k b s) -> p k b s", k=KT, s=S),
                                  mod_of(2 * n, c), ALU.mult).then_inc(xs_g_ready[n], 1)

            def ff_input_lo(T):
                if idle(T, FF):
                    return
                dve.wait_ge(ff_hi_ready, T - 1)
                dve.tensor_tensor(ff_lo[:], xs_g[1][:], ff_hi[:], ALU.subtract).then_inc(ff_lo_ready, 1)

            def hidden(T, j):
                if idle(T, FF):
                    return
                n = NJ * (T - 2) + j
                g, u = ps[:, GU_BANK[j], 0:TC], ps[:, GU_BANK[j], TC:2 * TC]
                dve.wait_ge(tanh_ready, n + 1)
                wait(dve, h_ready, n)
                dve.scalar_tensor_tensor(out=gate_s, in0=gate_t[:, j % 2, :], scalar=1.0, in1=g,
                                         op0=ALU.add, op1=ALU.mult).then_inc(gate_ready, 1)
                dve.wait_ge(gate_ready, n + 1)
                wait(dve, h_lo_ready, NJ * (T - 2) + max(j - 1, 0))
                dve.scalar_tensor_tensor(out=h_T[:, j % 2, :], in0=gate_s, scalar=0.5, in1=u,
                                         op0=ALU.mult, op1=ALU.mult).then_inc(h_ready, 1)

            def move_sum(T):
                if idle(T, FF):
                    return
                dve.wait_ge(sum_ready, T - 1)
                wait(dve, res_ready, T - 2)
                dve.tensor_copy(res_sum[:], sum_next[:]).then_inc(sum_moved, 1)

            def result(T):
                if idle(T, FF):
                    return
                dve.wait_ge(h_used, NJ * (T - 1))
                dve.wait_ge(sum_moved, T - 1)
                wait(dve, res_stored, 16 * (T - 2))
                dve.tensor_tensor(res[:].rearrange("p t f -> p (t f)"), ps[:, ACC_BANK, :],
                                  res_sum[:].rearrange("p t f -> p (t f)"), ALU.add).then_inc(res_ready, 1)

            def turn(T):
                input_lo(T, 0)
                set_up_mask(T)
                gain_in(T, 1)
                ff_input_lo(T)
                values(T, 1)
                hidden(T, 0)
                hidden(T, 1)
                values(T, 0)
                set_up_modulations(T)
                more_weights(T, 0)
                more_weights(T, 1)
                shift_scores(T, 0, 0)
                shift_scores(T, 0, 1)
                shift_scores(T, 0, 2)
                shift_scores(T, 0, 3)
                shift_scores(T, 1, 0)
                norm_output(T, 0, 0)
                hidden(T, 2)
                more_weights(T, 2)
                shift_scores(T, 1, 1)
                norm_output(T, 0, 1)
                shift_scores(T, 1, 2)
                output_lo(T, 0)
                shift_scores(T, 1, 3)
                hidden(T, 3)
                hidden(T, 4)
                more_weights(T, 3)
                more_weights(T, 4)
                modulate_y(T)
                norm_output(T, 1, 0)
                hidden(T, 5)
                move_sum(T)
                more_weights(T, 5)
                more_weights(T, 6)
                norm_output(T, 1, 1)
                norm_x(T, 0)
                output_lo(T, 1)
                more_weights(T, 7)
                gain_in(T, 0)
                hidden(T, 6)
                more_weights(T, 8)
                more_weights(T, 9)
                new_x2(T)
                hidden(T, 7)
                input_lo(T, 1)
                norm_x(T, 1)
                result(T)
                more_weights(T, 10)
                more_weights(T, 11)

            weights_lo(0, 1, 2)
            turn(0)
            turn(1)
            turn(2)
            with dve.Fori(3, NCH) as T:
                turn(T)
            turn(NCH)
            turn(NCH + 1)

        @block.tensor
        def _(pe):
            def modulations(T):
                if not first(T, L0):
                    return
                pe.wait_ge(silu_ready, 1)
                pe.matmul(ps[0:NB, 0, :], condT_silu[:], wcT[:], start=True, stop=True).then_inc(mod_ready, 1)
                for i in range(4 * KT):
                    mm = pe.matmul(ps[:, 1, NB * i:NB * i + NB],
                                   modw[i // KT][:, P * (i % KT):P * (i % KT) + P],
                                   condT[:], start=True, stop=True)
                mm.then_inc(mod_ready, 1)

            def bank_read(T, users):
                for s, lag, per, nth, turn in users if isinstance(T, int) else users[:1]:
                    wait(pe, s, done(T, lag, per, nth, turn))

            def split_product(dst, pairs, first=True, last=True):
                terms = [(x[i], y[j]) for x, y in pairs for i, j in ((0, 0), (0, 1), (1, 0))]
                for n, (x, y) in enumerate(terms):
                    mm = pe.matmul(dst, x, y, start=first and n == 0, stop=last and n == len(terms) - 1,
                                   skip_group_check=True)
                return mm

            def project_features(T, l, w, bank, ready, users):
                if idle(T, l):
                    return
                if first(T, l):
                    pe.wait_ge(w_lo_done, WCOL[w] // WBLK + 1)
                pe.wait_ge(in_lo_ready[l], T - l + 1)
                bank_read(T, users)
                for m in range(KT):
                    mm = split_product(ps[:, bank, TC * m:TC * m + TC],
                                       [(w_parts(w, k, P * m, P), (in_hi[l][:, k, :], in_lo[l][:, k, :]))
                                        for k in range(KT)], first=m == 0)
                mm.then_inc(ready, 1)

            def project_keys(T, l, *users):
                project_features(T, l, f"k{l}", KEYS_BANK[l], k_ready[l], users)

            def project_queries(T, l, *users):
                project_features(T, l, f"q{l}", QUERIES_BANK[l], q_ready[l], users)

            def project_values(T, l, *users):
                if idle(T, l):
                    return
                w = f"v{l}"
                if first(T, l):
                    pe.wait_ge(w_lo_done, WCOL[w] // WBLK + 1)
                bank_read(T, users)
                for t in range(NT):
                    rows = slice(P * t, P * t + P)
                    mm = split_product(ps[:, VALUES_BANK[l], D * t:D * t + D],
                                       [((in_hi[l][:, k, rows], in_lo[l][:, k, rows]), w_parts(w, k, 0, D))
                                        for k in range(KT)], first=t == 0)
                mm.then_inc(v_ready[l], 1)

            def scores(T, l, i, *users):
                if idle(T, l):
                    return
                t, m = divmod(i, KT)
                if i == 0:
                    pe.wait_ge(q_copied[l], T - l + 1)
                    pe.wait_ge(kdiag_landed[l], 16 * HH * (T - l + 1))
                    if first(T, L0):
                        pe.wait_ge(mask_ready, 1)
                        pe.wait_ge(sel_ready, 1)
                bank_read(T, users)
                out_bank = SCORES_BANK[l][i]
                if l == 0:
                    pe.matmul(ps[:, out_bank, :], seq_sel[:], mask_neg[:].rearrange("q h s -> q (h s)"),
                              start=True, stop=False, skip_group_check=True)
                for b in range(2):
                    at = S * (2 * t + b)
                    mm = pe.matmul(ps[S * b:S * b + S, out_bank, :], q_T[l][:, m, at:at + S],
                                   k_diag[l][:, m, :, at:at + S], start=l == 1, stop=True,
                                   skip_group_check=True)
                mm.then_inc(scores_ready[l], 1)

            def transpose_probs(T, l, i, *users):
                if idle(T, l):
                    return
                pe.wait_ge(probs_ready[l], NI * (T - l) + i + 1)
                bank_read(T, users)
                for j in range(4):
                    mm = pe.transpose(ps[:, PROBS_T_BANK[l][i], P * j:P * j + P],
                                      probs[:, i % 2, P * j:P * j + P], ident[:])
                mm.then_inc(pT_ready[l], 1)

            def weigh_values(T, l, i, *users):
                if idle(T, l):
                    return
                t, m = divmod(i, KT)
                pe.wait_ge(pT_copied[l], NI * (T - l) + i + 1)
                if i == 0:
                    pe.wait_ge(v_copied[l], T - l + 1)
                bank_read(T, users)
                for j in range(4):
                    pair = 4 * m + j
                    for b in range(2):
                        mm = pe.matmul(ps[S * b:S * b + S, OUT_BANK[l][t], 2 * DE * pair:2 * DE * (pair + 1)],
                                       probs_T[:, i % 2, P * j + S * b:P * j + S * b + S],
                                       v_pairs[l][:, t, b, pair, :], start=True, stop=True)
                mm.then_inc(pv_ready[l], 1)

            def transpose_output(T, l, *users):
                if idle(T, l):
                    return
                pe.wait_ge(o_ready[l], NT * (T - l + 1))
                bank_read(T, users)
                for t in range(NT):
                    for k in range(KT):
                        at = P * (KT * t + k)
                        mm = pe.transpose(ps[:, OUT_T_BANK[l], at:at + P], o_row[:, t, P * k:P * k + P],
                                          ident[:])
                mm.then_inc(oT_ready[l], 1)

            def output_product(T, l, *users):
                if idle(T, l):
                    return
                if first(T, l):
                    pe.wait_ge(w_lo_done, WCOL[f"o{l}"] // WBLK + 1)
                pe.wait_ge(o_lo_ready[l], T - l + 1)
                bank_read(T, users)
                for t in range(NT):
                    mm = split_product(ps[:, Y_BANK[l], D * t:D * t + D],
                                       [((o_hi[:, t, k, :], o_lo[:, t, k, :]), w_parts(f"o{l}", k, 0, D))
                                        for k in range(KT)], first=t == 0)
                mm.then_inc(y_ready[l], 1)

            def transpose_normed(T, n, *users):
                lag = (L0, FF)[n]
                if idle(T, lag):
                    return
                pe.wait_ge(xs_ready[n], T - lag + 1)
                bank_read(T, users)
                for k in range(KT):
                    for t in range(NT):
                        at = TC * k + P * t
                        mm = pe.transpose(ps[:, XS_T_BANK[n], at:at + P], xs_row[n][:, t, P * k:P * k + P],
                                          ident[:])
                mm.then_inc(xsT_ready[n], 1)

            def hidden_in(T, j, *users):
                if idle(T, FF):
                    return
                if j == 0:
                    pe.wait_ge(ff_lo_ready, T - 1)
                bank_read(T, users)
                for n, name in enumerate(("gate", "hid")):
                    mm = split_product(ps[:, GU_BANK[j], TC * n:TC * n + TC],
                                       [(w_parts(name, k, P * j, P, HID), (ff_hi[:, k, :], ff_lo[:, k, :]))
                                        for k in range(KT)], first=n == 0)
                mm.then_inc(gu_ready, 1)

            def hidden_out(T, j, *users):
                if idle(T, FF):
                    return
                pe.wait_ge(h_lo_ready, NJ * (T - 2) + j + 1)
                bank_read(T, users)
                for t in range(NT):
                    rows = slice(P * t, P * t + P)
                    mm = split_product(ps[:, ACC_BANK, D * t:D * t + D],
                                       [((h_hi[:, j % 2, rows], h_lo[:, j % 2, rows]),
                                         w_parts("out", j, 0, D))],
                                       first=j == 0 and t == 0, last=j == NJ - 1)
                mm.then_inc(h_used, 1)

            def turn(T):
                project_keys(T, 1, (o_lo_ready[1], L1, 1, 1, BEFORE), (pT_copied[0], L0, NI, 3, BEFORE))
                transpose_normed(T, 1, (h_ready, FF, NJ, 7, BEFORE))
                project_queries(T, 1, (pT_copied[1], L1, NI, 2, BEFORE), (o_lo_ready[0], L0, 1, 1, BEFORE))
                project_keys(T, 0, (k_copied[1], L1, 1, 1, NOW), (pT_copied[0], L0, NI, 3, BEFORE))
                project_queries(T, 0, (x2_ready, L1, 1, 1, BEFORE), (o_ready[0], L0, NT, 2, BEFORE))
                project_values(T, 1, (y_mod_ready, L0, 1, 1, BEFORE), (v_copied[1], L1, 1, 1, BEFORE))
                hidden_in(T, 0, (res_ready, FF, 1, 1, BEFORE))
                hidden_in(T, 1, (h_ready, FF, NJ, 8, BEFORE))
                project_values(T, 0, (v_copied[1], L1, 1, 1, NOW), (y_mod_ready, L0, 1, 1, BEFORE))
                modulations(T)
                hidden_in(T, 2, (xs_g_ready[1], FF, 1, 1, NOW))
                scores(T, 0, 0, (xs_g_ready[0], L0, 1, 1, BEFORE), (pT_copied[1], L1, NI, 3, BEFORE))
                scores(T, 0, 1, (q_copied[0], L0, 1, 1, NOW), (x2_ready, L1, 1, 1, BEFORE))
                scores(T, 0, 2, (k_copied[0], L0, 1, 1, NOW), (k_copied[1], L1, 1, 1, NOW))
                scores(T, 0, 3, (shifted_ready[0], L0, NI, 1, NOW), (pT_copied[1], L1, NI, 3, BEFORE))
                transpose_probs(T, 0, 0, (v_copied[0], L0, 1, 1, NOW), (v_copied[1], L1, 1, 1, NOW))
                scores(T, 1, 0, (shifted_ready[0], L0, NI, 2, NOW), (x2_ready, L1, 1, 1, BEFORE))
                transpose_probs(T, 0, 1, (q_copied[1], L1, 1, 1, NOW), (o_lo_ready[0], L0, 1, 1, BEFORE))
                hidden_out(T, 0, (h_ready, FF, NJ, 1, NOW))
                weigh_values(T, 0, 0, (pT_copied[0], L0, NI, 1, NOW), (v_copied[1], L1, 1, 1, NOW))
                transpose_probs(T, 0, 2, (shifted_ready[0], L0, NI, 3, NOW), (k_copied[1], L1, 1, 1, NOW))
                weigh_values(T, 0, 1)
                transpose_probs(T, 0, 3, (pT_copied[0], L0, NI, 2, NOW), (q_copied[1], L1, 1, 1, NOW))
                scores(T, 1, 1, (pT_copied[0], L0, NI, 3, NOW), (k_copied[1], L1, 1, 1, NOW))
                weigh_values(T, 0, 2, (shifted_ready[1], L1, NI, 1, NOW), (shifted_ready[0], L0, NI, 2, NOW))
                weigh_values(T, 0, 3)
                hidden_in(T, 3, (h_ready, FF, NJ, 2, NOW))
                scores(T, 1, 2, (shifted_ready[0], L0, NI, 4, NOW), (pT_copied[1], L1, NI, 3, BEFORE))
                transpose_output(T, 0, (pT_copied[0], L0, NI, 4, NOW), (q_copied[1], L1, 1, 1, NOW))
                transpose_probs(T, 1, 0, (o_ready[0], L0, NT, 2, NOW), (shifted_ready[1], L1, NI, 1, NOW))
                scores(T, 1, 3, (shifted_ready[1], L1, NI, 2, NOW), (pT_copied[0], L0, NI, 3, NOW))
                hidden_in(T, 4, (h_ready, FF, NJ, 3, NOW))
                output_product(T, 0, (o_ready[0], L0, NT, 1, NOW), (v_copied[1], L1, 1, 1, NOW))
                transpose_probs(T, 1, 1, (o_lo_ready[0], L0, 1, 1, NOW), (q_copied[1], L1, 1, 1, NOW))
                hidden_out(T, 1)
                weigh_values(T, 1, 0, (pT_copied[1], L1, NI, 1, NOW), (o_ready[0], L0, NT, 2, NOW))
                weigh_values(T, 1, 1)
                transpose_probs(T, 1, 2, (shifted_ready[1], L1, NI, 3, NOW), (shifted_ready[0], L0, NI, 4, NOW))
                transpose_probs(T, 1, 3, (shifted_ready[1], L1, NI, 4, NOW), (pT_copied[0], L0, NI, 3, NOW))
                hidden_in(T, 5, (h_ready, FF, NJ, 4, NOW))
                weigh_values(T, 1, 2, (pT_copied[1], L1, NI, 4, NOW), (pT_copied[0], L0, NI, 3, NOW))
                weigh_values(T, 1, 3)
                hidden_out(T, 2)
                hidden_in(T, 6, (h_ready, FF, NJ, 5, NOW))
                transpose_output(T, 1, (o_ready[1], L1, NT, 2, NOW), (pT_copied[0], L0, NI, 3, NOW))
                hidden_out(T, 3)
                hidden_in(T, 7, (h_ready, FF, NJ, 6, NOW))
                transpose_normed(T, 0, (pT_copied[1], L1, NI, 3, NOW), (shifted_ready[0], L0, NI, 4, NOW))
                output_product(T, 1, (o_ready[1], L1, NT, 1, NOW), (o_ready[0], L0, NT, 2, NOW))
                hidden_out(T, 4)
                hidden_out(T, 5)
                hidden_out(T, 6)
                hidden_out(T, 7)

            turn(0)
            turn(1)
            pe.wait_ge(w_lo_done, NWB)
            pe.wait_ge(modT_done, 1)
            turn(2)
            with pe.Fori(3, NCH) as T:
                turn(T)
            turn(NCH)
            turn(NCH + 1)


def kernel(**inputs):
    import numpy as np
    import concourse.bacc as bacc
    from concourse.bass_utils import run_bass_kernel_spmd

    def T(name):
        return np.asarray(inputs[name]).T

    def tiles(w):
        return w.reshape(-1, P, w.shape[1]).transpose(1, 0, 2).reshape(P, -1)

    def cols(name):
        return np.asarray(inputs[name]).reshape(KT, P).T

    names = ["L0_cond_Wk", "L0_cond_Wq", "L0_cond_Wv", "L0_cond_Wo", "L1_cond_Wk", "L1_cond_Wq",
             "L1_cond_Wv", "L1_cond_Wo", "L1_cond_gate_w", "L1_cond_hid_w", "L1_cond_out_w"]
    x = np.asarray(inputs["x"]).reshape(NCH, NT, P, D)
    arrays = {
        "x": x,
        "xT": x.reshape(NCH, TC, KT, P).transpose(0, 3, 2, 1),
        "weights": np.concatenate([tiles(T(n)) for n in names], axis=1),
        "condT": T("cond_256"),
        "wcT": T("L0_cond_Wc"),
        "bc": np.asarray(inputs["L0_cond_bc"]),
        "rms": np.asarray(inputs["L0_cond_rms_scale"]),
        "g1wT": T("L1_cond_g1w"), "b1wT": T("L1_cond_b1w"),
        "g2wT": T("L1_cond_g2w"), "b2wT": T("L1_cond_b2w"),
        "modb": np.concatenate([cols("L1_cond_" + n) for n in ("g1b", "b1b", "g2b", "b2b")], axis=1),
        "mask": np.asarray(inputs["mask_SxS_bk1"]),
    }
    arrays = {n: np.ascontiguousarray(v) for n, v in arrays.items()}

    nc = bacc.Bacc("TRN2", target_bir_lowering=False, num_devices=1)
    aps = {n: nc.dram_tensor(f"in_{n}", v.shape, mybir.dt.from_np(v.dtype), kind="ExternalInput").ap()
           for n, v in arrays.items()}
    out = nc.dram_tensor("out", (NCH, NT, P, D), F32, kind="ExternalOutput").ap()
    build(nc, aps, out)
    r = run_bass_kernel_spmd(nc, [{f"in_{n}": v for n, v in arrays.items()}], core_ids=[0])
    return r.results[0]["out"].reshape(NB, S, D)
```

```python
from contextlib import ExitStack

import concourse.bass as bass
from concourse import mybir

ALU = mybir.AluOpType
ACT = mybir.ActivationFunctionType
AXX = mybir.AxisListType.X
F32 = mybir.dt.float32
F32R = mybir.dt.float32r
I32 = mybir.dt.int32
U8 = mybir.dt.uint8
BF16 = mybir.dt.bfloat16

P = 128
NB, S, D = 32, 64, 256
H, DH = 16, 16
DT = 64
HID = 1024
KT = D // P
HH = H // KT
NP = H // 2
DE = DH + 1
NT = 2
TC = NT * P
NCH = NB * S // TC
CB = TC // S
NI = NT * KT
NJ = HID // P
EPS = 1e-6
SCALE = DH ** -0.5
BIG = 1e30
NEWTON = 3
CHAIN = 3 + 3 * NEWTON
ROOT_SEED = 0x5F3759DF

WCOL = {w: 512 * n for n, w in enumerate(["k0", "q0", "v0", "o0", "k1", "q1", "v1", "o1"])}
WCOL["gate"], WCOL["hid"], WCOL["out"] = 4096, 4096 + 2 * HID, 4096 + 4 * HID
WBLK = 512
NWB = (4096 + 6 * HID) // WBLK
NSTAGE = 3

L0, L1, FF = 0, 1, 2
NOW, BEFORE = 0, -1

GU_BANK = [0, 1, 2, 0, 2, 0, 2, 0]
ACC_BANK = 1
KEYS_BANK = [4, 3]
QUERIES_BANK = [5, 7]
VALUES_BANK = [4, 6]
SCORES_BANK = [[3, 7, 6, 3], [7, 4, 5, 7]]
PROBS_T_BANK = [[5, 4, 6, 3], [6, 5, 6, 3]]
OUT_BANK = [[5, 6], [7, 6]]
OUT_T_BANK = [3, 4]
Y_BANK = [4, 4]
XS_T_BANK = [7, 0]


def idle(T, lag):
    return isinstance(T, int) and not 0 <= T - lag < NCH


def first(T, lag):
    return isinstance(T, int) and T == lag


def done(T, lag, per, nth, turn=NOW):
    count = per * (T + turn - lag) + nth
    return min(count, per * NCH) if isinstance(T, int) else count


def wait(eng, s, count):
    if not (isinstance(count, int) and count <= 0):
        eng.wait_ge(s, count)


def weight_blocks(T, slot):
    if first(T, L0):
        return [3 + slot] if slot < 5 else []
    return [8 + slot] if first(T, L1) else []


def load_blocks(T, slot):
    return [n + NSTAGE for n in weight_blocks(T, slot) if n + NSTAGE < NWB]


def build(nc, a, out):
    ctx = ExitStack()
    with ctx:
        def sb(name, shape, dt=F32):
            return ctx.enter_context(nc.sbuf_tensor(name, shape, dt))

        def sem(name):
            return ctx.enter_context(nc.semaphore(name))

        ps = ctx.enter_context(nc.psum_tensor("ps", [P, 8, 512], F32))
        mod_dram = nc.dram_tensor("mod_rows_dram", [NB, 2 * D], F32, kind="Internal").ap()

        w_stage = sb("w_stage", [P, NSTAGE, WBLK])
        w_hi = sb("w_hi", [P, NWB * WBLK], F32R)
        w_lo = sb("w_lo", [P, NWB * WBLK], F32R)
        ident = sb("ident", [P, P])
        seq_sel = sb("seq_sel", [S, P], F32R)
        mask_u8 = sb("mask_u8", [S, S], U8)
        mask_neg = sb("mask_neg", [S, HH, S], F32R)
        condT = sb("condT", [DT, NB])
        condT_silu = sb("condT_silu", [DT, NB])
        modb = sb("modb", [P, 4 * KT])
        modT = sb("modT", [P, 4, KT, NB])

        x_T = sb("x_T", [P, KT, TC])
        x_row = sb("x_row", [P, NT, D])
        in_hi = [sb(f"in_hi{l}", [P, KT, TC], F32R) for l in range(2)]
        in_lo = [sb(f"in_lo{l}", [P, KT, TC], F32R) for l in range(2)]
        ff_hi = sb("ff_hi", [P, KT, TC], F32R)
        ff_lo = sb("ff_lo", [P, KT, TC], F32R)
        q_T = [sb(f"q_T{l}", [P, KT, TC]) for l in range(2)]
        k_T = [sb(f"k_T{l}", [P, KT, TC]) for l in range(2)]
        k_diag = [sb(f"k_diag{l}", [P, KT, HH, TC]) for l in range(2)]
        v_pairs = [sb(f"v_pairs{l}", [P, NT, 2, NP, 2 * DE]) for l in range(2)]
        row_max = [sb(f"row_max{l}", [P, HH]) for l in range(2)]
        shifted = sb("shifted", [P, 2, HH * S])
        probs = sb("probs", [P, 2, HH * S])
        probs_T = sb("probs_T", [P, 2, 4 * P])
        inv_sum = [sb(f"inv_sum{l}", [P, H]) for l in range(2)]
        o_row = sb("o_row", [P, NT, D])
        o_hi = sb("o_hi", [P, NT, KT, P], F32R)
        o_lo = sb("o_lo", [P, NT, KT, P], F32R)
        mod_tile = sb("mod_tile", [P, NT, 2 * D])
        y_mod = sb("y_mod", [P, NT, D])
        x1 = sb("x1", [P, NT, D])
        x1_kept = sb("x1_kept", [P, NT, D])
        x2 = sb("x2", [P, NT, D])
        sq_junk = sb("sq_junk", [P, 3, NT, D], BF16)
        sumsq = sb("sumsq", [P, 3, NT])
        mean_sq = sb("mean_sq", [P, 3, NT])
        root_bits = sb("root_bits", [P, 3, NT], I32)
        root = sb("root", [P, 3, NT])
        root_i = sb("root_i", [P, 3, NT], I32)
        root_a = sb("root_a", [P, 3, NT])
        root_b = sb("root_b", [P, 3, NT])
        xs_row = [sb(f"xs_row{n}", [P, NT, D]) for n in range(2)]
        xs_g = [sb(f"xs_g{n}", [P, KT, TC]) for n in range(2)]
        gate_t = w_stage[:, 0, :].rearrange("p (j s) -> p j s", j=2)
        h_T = w_stage[:, 1, :].rearrange("p (j s) -> p j s", j=2)
        gate_s = w_stage[:, 2, 0:TC]
        h_hi = sb("h_hi", [P, 2, TC], F32R)
        h_lo = sb("h_lo", [P, 2, TC], F32R)
        sum_next = sb("sum_next", [P, NT, D])
        res_sum = sb("res_sum", [P, NT, D])
        res = sb("res", [P, NT, D])
        wcT = x2[0:DT].rearrange("p t f -> p (t f)")
        bc_rows = sum_next[0:NB].rearrange("p t f -> p (t f)")
        mod_rows = res_sum[0:NB].rearrange("p t f -> p (t f)")
        rms_rows = res[0:NB, 0, :]
        modw = [t[0:DT, k, :] for t in xs_g for k in range(KT)]

        w_landed = [sem(f"w_landed{n}") for n in range(NSTAGE)]
        w_hi_done, w_lo_done = sem("w_hi_done"), sem("w_lo_done")
        consts_landed, pool_set = sem("consts_landed"), sem("pool_set")
        ident_ready, v_ones_set = sem("ident_ready"), sem("v_ones_set")
        sel_ready, mask_ready = sem("sel_ready"), sem("mask_ready")
        silu_ready, mod_ready = sem("silu_ready"), sem("mod_ready")
        mod_chain, modT_done, mod_stored = sem("mod_chain"), sem("modT_done"), sem("mod_stored")
        xT_landed, xrow_landed, modtile_landed = sem("xT_landed"), sem("xrow_landed"), sem("modtile_landed")
        res_stored = sem("res_stored")
        def by_layer(name):
            return [sem(f"{name}{l}") for l in range(2)]

        in_hi_ready, in_lo_ready = by_layer("in_hi_ready"), by_layer("in_lo_ready")
        k_ready, q_ready, v_ready = by_layer("k_ready"), by_layer("q_ready"), by_layer("v_ready")
        k_copied, q_copied, v_copied = by_layer("k_copied"), by_layer("q_copied"), by_layer("v_copied")
        kdiag_landed = by_layer("kdiag_landed")
        scores_ready, max_ready, max_clamped = by_layer("scores_ready"), by_layer("max_ready"), sem("max_clamped")
        shifted_ready, probs_ready = by_layer("shifted_ready"), by_layer("probs_ready")
        pT_ready, pT_copied = by_layer("pT_ready"), by_layer("pT_copied")
        pv_ready, inv_ready, o_ready = by_layer("pv_ready"), by_layer("inv_ready"), by_layer("o_ready")
        oT_ready, o_hi_ready, o_lo_ready = by_layer("oT_ready"), by_layer("o_hi_ready"), by_layer("o_lo_ready")
        y_ready = by_layer("y_ready")
        squared = [sem(f"squared{r}") for r in range(3)]
        newton = [sem(f"newton{r}") for r in range(3)]
        shift_ready, y_mod_ready = sem("shift_ready"), sem("y_mod_ready")
        x1_ready, x1_kept_ready, x2_ready = sem("x1_ready"), sem("x1_kept_ready"), sem("x2_ready")
        sum_ready, sum_moved = sem("sum_ready"), sem("sum_moved")
        xs_ready, xsT_ready = by_layer("xs_ready"), by_layer("xsT_ready")
        xs_g_ready, xs_gb_ready = by_layer("xs_g_ready"), by_layer("xs_gb_ready")
        ff_hi_ready, ff_lo_ready = sem("ff_hi_ready"), sem("ff_lo_ready")
        gu_ready, tanh_ready, gate_ready = sem("gu_ready"), sem("tanh_ready"), sem("gate_ready")
        h_ready, h_hi_ready, h_lo_ready = sem("h_ready"), sem("h_hi_ready"), sem("h_lo_ready")
        h_used, res_ready = sem("h_used"), sem("res_ready")

        block = ctx.enter_context(nc.Block())

        CONSTS = (
            (condT[:], a["condT"]), (wcT[:], a["wcT"]), (mask_u8[:], a["mask"]),
            (bc_rows[:], a["bc"].partition_broadcast(NB)),
            (rms_rows[:], a["rms"].partition_broadcast(NB)),
            (modw[0], a["g1wT"]), (modw[1], a["b1wT"]),
            (modw[2], a["g2wT"]), (modw[3], a["b2wT"]),
            (modb[:], a["modb"]),
        )

        def by_seq(t):
            return t.rearrange("p k (b s) -> p k b s", s=S)

        def mod_of(which, c):
            return modT[:, which, :, bass.ds(c * CB, CB)].unsqueeze(3).to_broadcast([P, KT, CB, S])

        def w_parts(name, k, c0, n, width=D):
            at = WCOL[name] + k * width + c0
            return w_hi[:, at:at + n], w_lo[:, at:at + n]

        @block.sync
        def _(sp):
            def load_w(n):
                wait(sp, w_hi_done, n - NSTAGE + 1)
                wait(sp, w_lo_done, n - NSTAGE + 1)
                sp.dma_start(w_stage[:, n % NSTAGE, :], a["weights"][:, n * WBLK:(n + 1) * WBLK])\
                    .then_inc(w_landed[n % NSTAGE], 16)

            def load_more(T, slot):
                for n in load_blocks(T, slot):
                    load_w(n)

            def load_tokens(T):
                wait(sp, in_lo_ready[0], T)
                sp.dma_start(x_T[:], a["xT"][bass.ds(T, 1)].rearrange("a p k s -> (a p) k s"))\
                    .then_inc(xT_landed, 16)

            def tokens(T):
                if not (idle(T, L0) or first(T, L0)):
                    load_tokens(T)

            def rows(T):
                if idle(T, L0):
                    return
                if first(T, L0):
                    sp.wait_ge(mod_stored, 16)
                wait(sp, x1_ready, T)
                sp.dma_start(x_row[:], a["x"][bass.ds(T, 1)].rearrange("a t p f -> (a p) t f"))\
                    .then_inc(xrow_landed, 16)
                wait(sp, y_mod_ready, T)
                for b in range(CB):
                    sp.dma_start(mod_tile[S * (b % 2):S * (b % 2) + S, b // 2, :],
                                 mod_dram[bass.ds(T * CB + b, 1)].rearrange("a n -> (a n)")
                                 .partition_broadcast(S)).then_inc(modtile_landed, 16)

            def keys(T, l):
                if idle(T, l):
                    return
                if first(T, l):
                    sp.wait_ge(pool_set, 2 + 2 * l)
                sp.wait_ge(k_copied[l], T - l + 1)
                for h in range(HH):
                    own = slice(DH * h, DH * h + DH)
                    sp.dma_start(k_diag[l][own, :, h, :], k_T[l][own, :, :]).then_inc(kdiag_landed[l], 16)

            def turn(T):
                tokens(T)
                keys(T, 0)
                keys(T, 1)
                rows(T)

            def first_turn(T):
                tokens(T)
                keys(T, 0)
                keys(T, 1)
                load_more(T, 0)
                load_more(T, 1)
                load_more(T, 2)
                rows(T)
                load_more(T, 3)
                load_more(T, 4)
                load_more(T, 5)
                load_more(T, 6)
                load_more(T, 7)
                load_more(T, 8)
                load_more(T, 9)
                load_more(T, 10)
                load_more(T, 11)

            def last_turn(T):
                keys(T, 0)
                tokens(T)
                keys(T, 1)
                rows(T)

            load_tokens(0)
            for n in range(NSTAGE):
                load_w(n)
            for dst, src in CONSTS:
                sp.dma_start(dst, src).then_inc(consts_landed, 16)
            for n in range(NSTAGE, 2 * NSTAGE):
                load_w(n)
            first_turn(0)
            first_turn(1)
            turn(2)
            with sp.Fori(3, NCH) as T:
                turn(T)
            last_turn(NCH)

        @block.gpsimd
        def _(pool):
            pool.memset(ident[:], 0.0).then_inc(pool_set, 1)
            pool.wait_ge(pool_set, 1)
            pool.affine_select(out=ident[:], in_=ident[:], compare_op=ALU.not_equal, fill=1.0,
                               base=0, pattern=[[-1, P]], channel_multiplier=1).then_inc(ident_ready, 1)
            for l in range(2):
                pool.memset(k_diag[l][:], 0.0).then_inc(pool_set, 1)
                pool.memset(v_pairs[l][:], 0.0).then_inc(pool_set, 1)
                pool.wait_ge(pool_set, 2 * l + 3)
                pool.memset(v_pairs[l][0:S, :, :, :, DH:DE], 1.0).then_inc(v_ones_set, 1)
                pool.wait_ge(v_ones_set, 2 * l + 1)
                pool.memset(v_pairs[l][S:P, :, :, :, DE + DH:2 * DE], 1.0).then_inc(v_ones_set, 1)
                pool.wait_ge(v_ones_set, 2 * l + 2)
                if l == 0:
                    pool.wait_ge(mod_chain, 3)
                    pool.dma_start(mod_dram, mod_rows[:]).then_inc(mod_stored, 16)

            def shift_in(T):
                if idle(T, L0):
                    return
                pool.wait_ge(xrow_landed, 16 * (T + 1))
                pool.wait_ge(modtile_landed, 16 * CB * (T + 1))
                pool.tensor_tensor(x_row[:], x_row[:], mod_tile[:, :, D:2 * D], ALU.add)\
                    .then_inc(shift_ready, 1)

            def new_x1(T):
                if idle(T, L0):
                    return
                pool.wait_ge(y_mod_ready, T + 1)
                pool.wait_ge(shift_ready, T + 1)
                wait(pool, x1_kept_ready, T)
                wait(pool, xs_ready[0], T)
                pool.tensor_tensor(x1[:], y_mod[:], x_row[:], ALU.add).then_inc(x1_ready, 1)

            def bias_in(T, n):
                lag = (L0, FF)[n]
                if idle(T, lag):
                    return
                pool.wait_ge(xs_g_ready[n], T - lag + 1)
                pool.tensor_tensor(by_seq(xs_g[n][:]), by_seq(xs_g[n][:]), mod_of(2 * n + 1, T - lag),
                                   ALU.add).then_inc(xs_gb_ready[n], 1)

            def sum_residuals(T):
                if idle(T, L1):
                    return
                pool.wait_ge(x2_ready, T)
                wait(pool, sum_moved, T - 1)
                pool.tensor_tensor(sum_next[:], x1_kept[:], x2[:], ALU.add).then_inc(sum_ready, 1)

            def store(T):
                if idle(T, FF):
                    return
                pool.wait_ge(res_ready, T - 1)
                pool.dma_start(out[bass.ds(T - 2, 1)].rearrange("a t p f -> (a p) t f"), res[:])\
                    .then_inc(res_stored, 16)

            def hidden_lo(T, j):
                if idle(T, FF):
                    return
                pool.wait_ge(h_hi_ready, NJ * (T - 2) + j + 1)
                pool.tensor_tensor(h_lo[:, j % 2, :], h_T[:, j % 2, :], h_hi[:, j % 2, :],
                                   ALU.subtract).then_inc(h_lo_ready, 1)

            def turn(T):
                bias_in(T, 1)
                hidden_lo(T, 0)
                shift_in(T)
                hidden_lo(T, 1)
                hidden_lo(T, 2)
                hidden_lo(T, 3)
                new_x1(T)
                hidden_lo(T, 4)
                hidden_lo(T, 5)
                hidden_lo(T, 6)
                bias_in(T, 0)
                hidden_lo(T, 7)
                sum_residuals(T)
                store(T)

            def first_turn(T):
                store(T)
                hidden_lo(T, 0)
                shift_in(T)
                hidden_lo(T, 1)
                hidden_lo(T, 2)
                hidden_lo(T, 3)
                hidden_lo(T, 4)
                new_x1(T)
                hidden_lo(T, 5)
                hidden_lo(T, 6)
                bias_in(T, 1)
                bias_in(T, 0)
                sum_residuals(T)
                hidden_lo(T, 7)

            def last_turn(T):
                bias_in(T, 1)
                hidden_lo(T, 0)
                shift_in(T)
                hidden_lo(T, 1)
                hidden_lo(T, 2)
                hidden_lo(T, 3)
                hidden_lo(T, 4)
                hidden_lo(T, 5)
                bias_in(T, 0)
                new_x1(T)
                hidden_lo(T, 6)
                hidden_lo(T, 7)
                sum_residuals(T)
                store(T)

            pool.wait_ge(modT_done, 1)
            first_turn(0)
            first_turn(1)
            turn(2)
            with pool.Fori(3, NCH) as T:
                turn(T)
            last_turn(NCH)
            last_turn(NCH + 1)
            pool.wait_ge(res_stored, 16 * NCH)

        @block.scalar
        def _(act):
            def weights_hi(*ns):
                for n in ns:
                    act.wait_ge(w_landed[n % NSTAGE], 16 * (n // NSTAGE + 1))
                    act.activation(w_hi[:, n * WBLK:(n + 1) * WBLK], w_stage[:, n % NSTAGE, :], ACT.Copy)\
                        .then_inc(w_hi_done, 1)

            def more_weights(T, slot):
                weights_hi(*weight_blocks(T, slot))

            def input_hi(T, l):
                if idle(T, L0):
                    return
                if l == 0:
                    act.wait_ge(xT_landed, 16 * (T + 1))
                    wait(act, v_ready[0], T)
                else:
                    act.wait_ge(xs_gb_ready[0], T + 1)
                    wait(act, v_ready[1], T)
                act.activation(in_hi[l][:], (x_T if l == 0 else xs_g[0])[:], ACT.Copy)\
                    .then_inc(in_hi_ready[l], 1)

            def condition(T):
                if first(T, L0):
                    act.wait_ge(consts_landed, 16 * len(CONSTS))
                    act.activation(condT_silu[:], condT[:], ACT.Silu).then_inc(silu_ready, 1)

            def ff_input_hi(T):
                if idle(T, FF):
                    return
                act.wait_ge(xs_gb_ready[1], T - 1)
                wait(act, gu_ready, NJ * (T - 2))
                act.activation(ff_hi[:], xs_g[1][:], ACT.Copy).then_inc(ff_hi_ready, 1)

            def copy_keys(T, l):
                if idle(T, l):
                    return
                act.wait_ge(k_ready[l], T - l + 1)
                wait(act, kdiag_landed[l], 16 * HH * (T - l))
                act.activation(k_T[l][:], ps[:, KEYS_BANK[l], :], ACT.Copy).then_inc(k_copied[l], 1)

            def copy_queries(T, l):
                if idle(T, l):
                    return
                act.wait_ge(q_ready[l], T - l + 1)
                act.activation(q_T[l][:], ps[:, QUERIES_BANK[l], :], ACT.Copy).then_inc(q_copied[l], 1)

            def exponentials(T, l, i):
                if idle(T, l):
                    return
                act.wait_ge(shifted_ready[l], NI * (T - l) + i + 1)
                if i >= 2:
                    act.wait_ge(pT_ready[l], NI * (T - l) + i - 1)
                elif l == 0:
                    wait(act, pT_ready[1], done(T, L1, NI, i + 3, BEFORE))
                else:
                    wait(act, pT_ready[0], done(T, L0, NI, i + 3))
                if isinstance(T, int) and i < 2:
                    wait(act, pT_ready[l], done(T, l, NI, i + 3, BEFORE))
                act.activation(probs[:, i % 2, :], shifted[:, i % 2, :], ACT.Exp, scale=SCALE)\
                    .then_inc(probs_ready[l], 1)

            def copy_pT(T, l, i):
                if idle(T, l):
                    return
                act.wait_ge(pT_ready[l], NI * (T - l) + i + 1)
                if i >= 2:
                    act.wait_ge(pv_ready[l], NI * (T - l) + i - 1)
                elif l == 0:
                    wait(act, pv_ready[1], done(T, L1, NI, i + 3, BEFORE))
                else:
                    wait(act, pv_ready[0], done(T, L0, NI, i + 3))
                if isinstance(T, int) and i < 2:
                    wait(act, pv_ready[l], done(T, l, NI, i + 3, BEFORE))
                act.activation(probs_T[:, i % 2, :], ps[:, PROBS_T_BANK[l][i], :], ACT.Copy)\
                    .then_inc(pT_copied[l], 1)

            def output_hi(T, l):
                if idle(T, l):
                    return
                act.wait_ge(oT_ready[l], T - l + 1)
                wait(act, y_ready[1 - l], done(T, 1 - l, 1, 1, BEFORE if l == 0 else NOW))
                if isinstance(T, int):
                    wait(act, y_ready[l], T - l)
                act.activation(o_hi[:], ps[:, OUT_T_BANK[l], :], ACT.Copy).then_inc(o_hi_ready[l], 1)

            def squares(r, src):
                for t in range(NT):
                    ins = act.activation(sq_junk[:, r, t, :], src(t), ACT.Square,
                                         accum_out=sumsq[:, r, t:t + 1])
                ins.then_inc(squared[r], 1)

            def squares_y(T):
                if idle(T, L0):
                    return
                act.wait_ge(y_ready[0], T + 1)
                wait(act, y_mod_ready, T)
                squares(0, lambda t: ps[:, Y_BANK[0], D * t:D * t + D])

            def squares_x(T, n):
                if idle(T, n):
                    return
                act.wait_ge((x1_ready, x2_ready)[n], T - n + 1)
                wait(act, xs_ready[n], T - n)
                squares(1 + n, lambda t: (x1, x2)[n][:, t, :])

            def keep_x1(T):
                if idle(T, L1):
                    return
                act.wait_ge(x1_ready, T)
                wait(act, sum_ready, T - 1)
                act.activation(x1_kept[:], x1[:], ACT.Copy).then_inc(x1_kept_ready, 1)

            def tanh(T, j):
                if idle(T, FF):
                    return
                act.wait_ge(gu_ready, NJ * (T - 2) + j + 1)
                wait(act, gate_ready, NJ * (T - 2) + max(j - 1, 0))
                act.activation(gate_t[:, j % 2, :], ps[:, GU_BANK[j], 0:TC], ACT.Tanh, scale=0.5)\
                    .then_inc(tanh_ready, 1)

            def hidden_hi(T, j):
                if idle(T, FF):
                    return
                act.wait_ge(h_ready, NJ * (T - 2) + j + 1)
                wait(act, h_used, NJ * (T - 2) + j - 1)
                act.activation(h_hi[:, j % 2, :], h_T[:, j % 2, :], ACT.Copy).then_inc(h_hi_ready, 1)

            def turn(T):
                input_hi(T, 0)
                copy_keys(T, 0)
                ff_input_hi(T)
                copy_queries(T, 1)
                copy_keys(T, 1)
                tanh(T, 0)
                keep_x1(T)
                copy_queries(T, 0)
                hidden_hi(T, 0)
                tanh(T, 1)
                tanh(T, 2)
                tanh(T, 3)
                exponentials(T, 0, 0)
                exponentials(T, 0, 1)
                hidden_hi(T, 1)
                exponentials(T, 0, 2)
                copy_pT(T, 0, 0)
                copy_pT(T, 0, 1)
                exponentials(T, 0, 3)
                copy_pT(T, 0, 2)
                copy_pT(T, 0, 3)
                exponentials(T, 1, 0)
                output_hi(T, 0)
                tanh(T, 4)
                hidden_hi(T, 2)
                exponentials(T, 1, 1)
                squares_y(T)
                exponentials(T, 1, 2)
                hidden_hi(T, 3)
                copy_pT(T, 1, 0)
                exponentials(T, 1, 3)
                copy_pT(T, 1, 1)
                copy_pT(T, 1, 2)
                copy_pT(T, 1, 3)
                tanh(T, 5)
                squares_x(T, 0)
                hidden_hi(T, 4)
                output_hi(T, 1)
                tanh(T, 6)
                hidden_hi(T, 5)
                hidden_hi(T, 6)
                tanh(T, 7)
                hidden_hi(T, 7)
                input_hi(T, 1)
                squares_x(T, 1)

            def first_turn(T):
                tanh(T, 0)
                input_hi(T, 0)
                condition(T)
                copy_keys(T, 0)
                copy_keys(T, 1)
                tanh(T, 1)
                more_weights(T, 0)
                more_weights(T, 1)
                copy_queries(T, 0)
                copy_queries(T, 1)
                more_weights(T, 2)
                hidden_hi(T, 0)
                exponentials(T, 0, 0)
                copy_pT(T, 0, 0)
                exponentials(T, 0, 1)
                exponentials(T, 0, 2)
                hidden_hi(T, 1)
                copy_pT(T, 0, 1)
                exponentials(T, 0, 3)
                copy_pT(T, 0, 2)
                copy_pT(T, 0, 3)
                hidden_hi(T, 2)
                exponentials(T, 1, 0)
                tanh(T, 2)
                more_weights(T, 3)
                exponentials(T, 1, 1)
                keep_x1(T)
                hidden_hi(T, 3)
                more_weights(T, 4)
                output_hi(T, 0)
                copy_pT(T, 1, 0)
                hidden_hi(T, 4)
                tanh(T, 3)
                exponentials(T, 1, 2)
                more_weights(T, 5)
                tanh(T, 4)
                squares_y(T)
                more_weights(T, 6)
                exponentials(T, 1, 3)
                copy_pT(T, 1, 1)
                more_weights(T, 7)
                copy_pT(T, 1, 2)
                tanh(T, 5)
                copy_pT(T, 1, 3)
                more_weights(T, 8)
                hidden_hi(T, 5)
                hidden_hi(T, 6)
                squares_x(T, 0)
                tanh(T, 6)
                more_weights(T, 9)
                output_hi(T, 1)
                more_weights(T, 10)
                input_hi(T, 1)
                tanh(T, 7)
                more_weights(T, 11)
                hidden_hi(T, 7)
                squares_x(T, 1)
                ff_input_hi(T)

            def last_turn(T):
                exponentials(T, 0, 0)
                copy_keys(T, 1)
                copy_queries(T, 1)
                ff_input_hi(T)
                copy_keys(T, 0)
                exponentials(T, 0, 1)
                input_hi(T, 1)
                tanh(T, 0)
                exponentials(T, 0, 2)
                output_hi(T, 0)
                hidden_hi(T, 0)
                exponentials(T, 0, 3)
                tanh(T, 1)
                tanh(T, 2)
                exponentials(T, 1, 0)
                squares_y(T)
                hidden_hi(T, 1)
                copy_pT(T, 0, 0)
                keep_x1(T)
                exponentials(T, 1, 1)
                copy_pT(T, 0, 1)
                tanh(T, 3)
                copy_pT(T, 0, 2)
                hidden_hi(T, 2)
                tanh(T, 4)
                hidden_hi(T, 3)
                input_hi(T, 0)
                copy_pT(T, 0, 3)
                copy_pT(T, 1, 0)
                exponentials(T, 1, 2)
                squares_x(T, 0)
                copy_pT(T, 1, 1)
                exponentials(T, 1, 3)
                copy_pT(T, 1, 2)
                copy_pT(T, 1, 3)
                tanh(T, 5)
                output_hi(T, 1)
                hidden_hi(T, 4)
                copy_queries(T, 0)
                tanh(T, 6)
                hidden_hi(T, 5)
                tanh(T, 7)
                hidden_hi(T, 6)
                squares_x(T, 1)
                hidden_hi(T, 7)

            weights_hi(0, 1, 2)
            first_turn(0)
            first_turn(1)
            turn(2)
            with act.Fori(3, NCH) as T:
                turn(T)
            last_turn(NCH)
            last_turn(NCH + 1)

        @block.vector
        def _(dve):
            def set_up_mask(T):
                if not first(T, L0):
                    return
                dve.wait_ge(consts_landed, 16 * len(CONSTS))
                dve.tensor_scalar(mask_neg[:], mask_u8[:].unsqueeze(1).to_broadcast([S, HH, S]), -BIG,
                                  None, ALU.mult).then_inc(mask_ready, 1)
                dve.wait_ge(ident_ready, 1)
                dve.tensor_copy(seq_sel[:].rearrange("q (a r) -> q a r", a=2),
                                ident[0:S, 0:S].unsqueeze(1).to_broadcast([S, 2, S])).then_inc(sel_ready, 1)

            def set_up_modulations(T):
                if not first(T, L0):
                    return
                dve.wait_ge(mod_ready, 1)
                dve.tensor_tensor(mod_rows[:, D:2 * D], ps[0:NB, 0, 0:D], bc_rows[:, 0:D], ALU.add)\
                    .then_inc(mod_chain, 1)
                dve.tensor_tensor(mod_rows[:, 0:D], ps[0:NB, 0, D:2 * D], bc_rows[:, D:2 * D], ALU.add)\
                    .then_inc(mod_chain, 1)
                dve.wait_ge(mod_chain, 2)
                dve.scalar_tensor_tensor(out=mod_rows[:, 0:D], in0=mod_rows[:, 0:D], scalar=1.0,
                                         in1=rms_rows[:], op0=ALU.add, op1=ALU.mult).then_inc(mod_chain, 1)
                dve.wait_ge(mod_ready, 2)
                dve.tensor_tensor(modT[:].rearrange("p w k b -> p (w k) b"),
                                  ps[:, 1, 0:4 * KT * NB].rearrange("p (i b) -> p i b", b=NB),
                                  modb[:].unsqueeze(2).to_broadcast([P, 4 * KT, NB]), ALU.add)\
                    .then_inc(modT_done, 1)

            def weights_lo(*ns):
                for n in ns:
                    dve.wait_ge(w_hi_done, n + 1)
                    dve.tensor_tensor(w_lo[:, n * WBLK:(n + 1) * WBLK], w_stage[:, n % NSTAGE, :],
                                      w_hi[:, n * WBLK:(n + 1) * WBLK], ALU.subtract).then_inc(w_lo_done, 1)

            def more_weights(T, slot):
                weights_lo(*weight_blocks(T, slot))

            def input_lo(T, l):
                if idle(T, L0):
                    return
                dve.wait_ge(in_hi_ready[l], T + 1)
                dve.tensor_tensor(in_lo[l][:], (x_T if l == 0 else xs_g[0])[:], in_hi[l][:], ALU.subtract)\
                    .then_inc(in_lo_ready[l], 1)

            def values(T, l):
                if idle(T, l):
                    return
                if first(T, l):
                    dve.wait_ge(v_ones_set, 2 * l + 2)
                dve.wait_ge(v_ready[l], T - l + 1)
                for par in range(2):
                    for b in range(2):
                        ins = dve.tensor_copy(
                            v_pairs[l][S * par:S * par + S, :, b, :, DE * par:DE * par + DH],
                            ps[S * b:S * b + S, VALUES_BANK[l], :].rearrange(
                                "p (t j e d) -> p t j e d", t=NT, j=NP, e=2)[:, :, :, par, :])
                ins.then_inc(v_copied[l], 1)

            def shift_scores(T, l, i):
                if idle(T, l):
                    return
                n = NI * (T - l) + i
                scores = ps[:, SCORES_BANK[l][i], :].rearrange("p (h s) -> p h s", s=S)
                dve.wait_ge(scores_ready[l], n + 1)
                wait(dve, shifted_ready[l], n)
                dve.tensor_reduce(row_max[l][:], scores, AXX, ALU.max).then_inc(max_ready[l], 1)
                dve.wait_ge(max_ready[l], n + 1)
                if l == 0:
                    dve.tensor_scalar(row_max[l][:], row_max[l][:], -BIG / 2, None, ALU.max)\
                        .then_inc(max_clamped, 1)
                    dve.wait_ge(max_clamped, n + 1)
                if i >= 2:
                    dve.wait_ge(probs_ready[l], n - 1)
                elif l == 0:
                    wait(dve, probs_ready[1], done(T, L1, NI, i + 3, BEFORE))
                else:
                    wait(dve, probs_ready[0], done(T, L0, NI, i + 3))
                if isinstance(T, int) and i < 2:
                    wait(dve, probs_ready[l], done(T, l, NI, i + 3, BEFORE))
                dve.tensor_tensor(shifted[:, i % 2, :].rearrange("p (h s) -> p h s", s=S), scores,
                                  row_max[l][:].unsqueeze(2).to_broadcast([P, HH, S]), ALU.subtract)\
                    .then_inc(shifted_ready[l], 1)

            def norm_output(T, l, t):
                if idle(T, l):
                    return
                n = NT * (T - l) + t
                sums = ps[:, OUT_BANK[l][t], 0:H * DE].rearrange("p (h e) -> p h e", e=DE)
                dve.wait_ge(pv_ready[l], NI * (T - l) + KT * t + KT)
                wait(dve, o_ready[l], n)
                if t == 0:
                    wait(dve, oT_ready[1 - l], done(T, 1 - l, 1, 1, BEFORE if l == 0 else NOW))
                    if isinstance(T, int):
                        wait(dve, oT_ready[l], T - l)
                dve.reciprocal(inv_sum[l][:], sums[:, :, DH]).then_inc(inv_ready[l], 1)
                dve.wait_ge(inv_ready[l], n + 1)
                dve.tensor_tensor(o_row[:, t, :].rearrange("p (h d) -> p h d", d=DH), sums[:, :, 0:DH],
                                  inv_sum[l][:].unsqueeze(2).to_broadcast([P, H, DH]), ALU.mult)\
                    .then_inc(o_ready[l], 1)

            def output_lo(T, l):
                if idle(T, l):
                    return
                dve.wait_ge(o_hi_ready[l], T - l + 1)
                dve.tensor_tensor(o_lo[:].rearrange("p t k s -> p (t k s)"), ps[:, OUT_T_BANK[l], :],
                                  o_hi[:].rearrange("p t k s -> p (t k s)"), ALU.subtract)\
                    .then_inc(o_lo_ready[l], 1)

            def inverse_root(c, r):
                at = [CHAIN * c]

                def link(ins):
                    at[0] = at[0] + 1
                    ins.then_inc(newton[r], 1)
                    dve.wait_ge(newton[r], at[0])

                m, bits, guess, y = mean_sq[:, r, :], root_bits[:, r, :], root_i[:, r, :], root[:, r, :]
                dve.wait_ge(squared[r], c + 1)
                link(dve.tensor_scalar(m, sumsq[:, r, :], 1.0 / D, EPS, ALU.mult, ALU.add))
                link(dve.tensor_scalar(bits, m.bitcast(I32), 1, None, ALU.logical_shift_right))
                link(dve.tensor_scalar(guess, bits, -1, ROOT_SEED, ALU.mult, ALU.add))
                for k in range(NEWTON):
                    y0 = guess.bitcast(F32) if k == 0 else y
                    link(dve.tensor_tensor(root_a[:, r, :], y0, y0, ALU.mult))
                    link(dve.scalar_tensor_tensor(out=root_b[:, r, :], in0=root_a[:, r, :], scalar=-0.5,
                                                  in1=m, op0=ALU.mult, op1=ALU.mult))
                    link(dve.scalar_tensor_tensor(out=y, in0=root_b[:, r, :], scalar=1.5, in1=y0,
                                                  op0=ALU.add, op1=ALU.mult))

            def modulate_y(T):
                if idle(T, L0):
                    return
                wait(dve, y_mod_ready, T)
                inverse_root(T, 0)
                dve.wait_ge(modtile_landed, 16 * CB * (T + 1))
                wait(dve, x1_ready, T)
                for t in range(NT):
                    ins = dve.scalar_tensor_tensor(
                        out=y_mod[:, t, :], in0=ps[:, Y_BANK[0], D * t:D * t + D],
                        scalar=root[:, 0, t:t + 1], in1=mod_tile[:, t, 0:D], op0=ALU.mult, op1=ALU.mult)
                ins.then_inc(y_mod_ready, 1)

            def new_x2(T):
                if idle(T, L1):
                    return
                dve.wait_ge(y_ready[1], T)
                dve.wait_ge(x1_kept_ready, T)
                wait(dve, sum_ready, T - 1)
                wait(dve, xs_ready[1], T - 1)
                dve.tensor_tensor(x2[:].rearrange("p t f -> p (t f)"), ps[:, Y_BANK[1], :],
                                  x1_kept[:].rearrange("p t f -> p (t f)"), ALU.add).then_inc(x2_ready, 1)

            def norm_x(T, n):
                if idle(T, n):
                    return
                wait(dve, xs_ready[n], T - n)
                inverse_root(T - n, 1 + n)
                wait(dve, xsT_ready[n], T - n)
                for t in range(NT):
                    ins = dve.tensor_scalar(xs_row[n][:, t, :], (x1, x2)[n][:, t, :],
                                            root[:, 1 + n, t:t + 1], None, ALU.mult)
                ins.then_inc(xs_ready[n], 1)

            def gain_in(T, n):
                c = T - (L0, FF)[n]
                if idle(T, (L0, FF)[n]):
                    return
                dve.wait_ge(xsT_ready[n], c + 1)
                wait(dve, (in_lo_ready[1], ff_lo_ready)[n], c)
                dve.tensor_tensor(by_seq(xs_g[n][:]),
                                  ps[:, XS_T_BANK[n], :].rearrange("p (k b s) -> p k b s", k=KT, s=S),
                                  mod_of(2 * n, c), ALU.mult).then_inc(xs_g_ready[n], 1)

            def ff_input_lo(T):
                if idle(T, FF):
                    return
                dve.wait_ge(ff_hi_ready, T - 1)
                dve.tensor_tensor(ff_lo[:], xs_g[1][:], ff_hi[:], ALU.subtract).then_inc(ff_lo_ready, 1)

            def hidden(T, j):
                if idle(T, FF):
                    return
                n = NJ * (T - 2) + j
                g, u = ps[:, GU_BANK[j], 0:TC], ps[:, GU_BANK[j], TC:2 * TC]
                dve.wait_ge(tanh_ready, n + 1)
                wait(dve, h_ready, n)
                dve.scalar_tensor_tensor(out=gate_s, in0=gate_t[:, j % 2, :], scalar=1.0, in1=g,
                                         op0=ALU.add, op1=ALU.mult).then_inc(gate_ready, 1)
                dve.wait_ge(gate_ready, n + 1)
                wait(dve, h_lo_ready, NJ * (T - 2) + max(j - 1, 0))
                dve.scalar_tensor_tensor(out=h_T[:, j % 2, :], in0=gate_s, scalar=0.5, in1=u,
                                         op0=ALU.mult, op1=ALU.mult).then_inc(h_ready, 1)

            def move_sum(T):
                if idle(T, FF):
                    return
                dve.wait_ge(sum_ready, T - 1)
                wait(dve, res_ready, T - 2)
                dve.tensor_copy(res_sum[:], sum_next[:]).then_inc(sum_moved, 1)

            def result(T):
                if idle(T, FF):
                    return
                dve.wait_ge(h_used, NJ * (T - 1))
                dve.wait_ge(sum_moved, T - 1)
                wait(dve, res_stored, 16 * (T - 2))
                dve.tensor_tensor(res[:].rearrange("p t f -> p (t f)"), ps[:, ACC_BANK, :],
                                  res_sum[:].rearrange("p t f -> p (t f)"), ALU.add).then_inc(res_ready, 1)

            def turn(T):
                input_lo(T, 0)
                move_sum(T)
                gain_in(T, 1)
                ff_input_lo(T)
                hidden(T, 0)
                values(T, 0)
                values(T, 1)
                hidden(T, 1)
                shift_scores(T, 0, 0)
                shift_scores(T, 0, 1)
                shift_scores(T, 0, 2)
                shift_scores(T, 0, 3)
                shift_scores(T, 1, 0)
                hidden(T, 2)
                norm_output(T, 0, 0)
                hidden(T, 3)
                norm_output(T, 0, 1)
                shift_scores(T, 1, 1)
                output_lo(T, 0)
                shift_scores(T, 1, 2)
                shift_scores(T, 1, 3)
                modulate_y(T)
                hidden(T, 4)
                norm_output(T, 1, 0)
                hidden(T, 5)
                norm_output(T, 1, 1)
                norm_x(T, 0)
                hidden(T, 6)
                output_lo(T, 1)
                gain_in(T, 0)
                hidden(T, 7)
                new_x2(T)
                input_lo(T, 1)
                norm_x(T, 1)
                result(T)

            def first_turn(T):
                input_lo(T, 0)
                set_up_mask(T)
                values(T, 0)
                set_up_modulations(T)
                more_weights(T, 0)
                more_weights(T, 1)
                values(T, 1)
                result(T)
                hidden(T, 0)
                shift_scores(T, 0, 0)
                shift_scores(T, 0, 1)
                shift_scores(T, 0, 2)
                ff_input_lo(T)
                hidden(T, 1)
                shift_scores(T, 0, 3)
                more_weights(T, 2)
                shift_scores(T, 1, 0)
                norm_output(T, 0, 0)
                hidden(T, 2)
                shift_scores(T, 1, 1)
                norm_output(T, 0, 1)
                more_weights(T, 3)
                hidden(T, 3)
                shift_scores(T, 1, 2)
                output_lo(T, 0)
                more_weights(T, 4)
                shift_scores(T, 1, 3)
                hidden(T, 4)
                more_weights(T, 5)
                move_sum(T)
                gain_in(T, 1)
                modulate_y(T)
                more_weights(T, 6)
                hidden(T, 5)
                norm_output(T, 1, 0)
                more_weights(T, 7)
                hidden(T, 6)
                norm_output(T, 1, 1)
                norm_x(T, 0)
                more_weights(T, 8)
                hidden(T, 7)
                output_lo(T, 1)
                gain_in(T, 0)
                more_weights(T, 9)
                more_weights(T, 10)
                input_lo(T, 1)
                new_x2(T)
                more_weights(T, 11)
                norm_x(T, 1)

            def last_turn(T):
                gain_in(T, 1)
                values(T, 0)
                shift_scores(T, 0, 0)
                modulate_y(T)
                move_sum(T)
                shift_scores(T, 0, 1)
                shift_scores(T, 0, 2)
                ff_input_lo(T)
                values(T, 1)
                hidden(T, 0)
                shift_scores(T, 0, 3)
                output_lo(T, 0)
                hidden(T, 1)
                norm_output(T, 0, 0)
                norm_x(T, 0)
                shift_scores(T, 1, 0)
                hidden(T, 2)
                shift_scores(T, 1, 1)
                norm_output(T, 0, 1)
                input_lo(T, 1)
                shift_scores(T, 1, 2)
                hidden(T, 3)
                shift_scores(T, 1, 3)
                hidden(T, 4)
                norm_output(T, 1, 0)
                norm_output(T, 1, 1)
                hidden(T, 5)
                output_lo(T, 1)
                input_lo(T, 0)
                hidden(T, 6)
                new_x2(T)
                hidden(T, 7)
                gain_in(T, 0)
                norm_x(T, 1)
                result(T)

            weights_lo(0, 1, 2)
            first_turn(0)
            first_turn(1)
            turn(2)
            with dve.Fori(3, NCH) as T:
                turn(T)
            last_turn(NCH)
            last_turn(NCH + 1)

        @block.tensor
        def _(pe):
            def modulations(T):
                if not first(T, L0):
                    return
                pe.wait_ge(silu_ready, 1)
                pe.matmul(ps[0:NB, 0, :], condT_silu[:], wcT[:], start=True, stop=True).then_inc(mod_ready, 1)
                for i in range(4 * KT):
                    mm = pe.matmul(ps[:, 1, NB * i:NB * i + NB],
                                   modw[i // KT][:, P * (i % KT):P * (i % KT) + P],
                                   condT[:], start=True, stop=True)
                mm.then_inc(mod_ready, 1)

            def bank_read(T, users):
                for s, lag, per, nth, turn in users if isinstance(T, int) else users[:1]:
                    wait(pe, s, done(T, lag, per, nth, turn))

            def split_product(dst, pairs, first=True, last=True):
                terms = [(x[i], y[j]) for x, y in pairs for i, j in ((0, 0), (0, 1), (1, 0))]
                for n, (x, y) in enumerate(terms):
                    mm = pe.matmul(dst, x, y, start=first and n == 0, stop=last and n == len(terms) - 1,
                                   skip_group_check=True)
                return mm

            def project_features(T, l, w, bank, ready, users):
                if idle(T, l):
                    return
                if first(T, l):
                    pe.wait_ge(w_lo_done, WCOL[w] // WBLK + 1)
                pe.wait_ge(in_lo_ready[l], T - l + 1)
                bank_read(T, users)
                for m in range(KT):
                    mm = split_product(ps[:, bank, TC * m:TC * m + TC],
                                       [(w_parts(w, k, P * m, P), (in_hi[l][:, k, :], in_lo[l][:, k, :]))
                                        for k in range(KT)], first=m == 0)
                mm.then_inc(ready, 1)

            def project_keys(T, l, *users):
                project_features(T, l, f"k{l}", KEYS_BANK[l], k_ready[l], users)

            def project_queries(T, l, *users):
                project_features(T, l, f"q{l}", QUERIES_BANK[l], q_ready[l], users)

            def project_values(T, l, *users):
                if idle(T, l):
                    return
                w = f"v{l}"
                if first(T, l):
                    pe.wait_ge(w_lo_done, WCOL[w] // WBLK + 1)
                bank_read(T, users)
                for t in range(NT):
                    rows = slice(P * t, P * t + P)
                    mm = split_product(ps[:, VALUES_BANK[l], D * t:D * t + D],
                                       [((in_hi[l][:, k, rows], in_lo[l][:, k, rows]), w_parts(w, k, 0, D))
                                        for k in range(KT)], first=t == 0)
                mm.then_inc(v_ready[l], 1)

            def scores(T, l, i, *users):
                if idle(T, l):
                    return
                t, m = divmod(i, KT)
                if i == 0:
                    pe.wait_ge(q_copied[l], T - l + 1)
                    pe.wait_ge(kdiag_landed[l], 16 * HH * (T - l + 1))
                    if first(T, L0):
                        pe.wait_ge(mask_ready, 1)
                        pe.wait_ge(sel_ready, 1)
                bank_read(T, users)
                out_bank = SCORES_BANK[l][i]
                if l == 0:
                    pe.matmul(ps[:, out_bank, :], seq_sel[:], mask_neg[:].rearrange("q h s -> q (h s)"),
                              start=True, stop=False, skip_group_check=True)
                for b in range(2):
                    at = S * (2 * t + b)
                    mm = pe.matmul(ps[S * b:S * b + S, out_bank, :], q_T[l][:, m, at:at + S],
                                   k_diag[l][:, m, :, at:at + S], start=l == 1, stop=True,
                                   skip_group_check=True)
                mm.then_inc(scores_ready[l], 1)

            def transpose_probs(T, l, i, *users):
                if idle(T, l):
                    return
                pe.wait_ge(probs_ready[l], NI * (T - l) + i + 1)
                bank_read(T, users)
                for j in range(4):
                    mm = pe.transpose(ps[:, PROBS_T_BANK[l][i], P * j:P * j + P],
                                      probs[:, i % 2, P * j:P * j + P], ident[:])
                mm.then_inc(pT_ready[l], 1)

            def weigh_values(T, l, i, *users):
                if idle(T, l):
                    return
                t, m = divmod(i, KT)
                pe.wait_ge(pT_copied[l], NI * (T - l) + i + 1)
                if i == 0:
                    pe.wait_ge(v_copied[l], T - l + 1)
                bank_read(T, users)
                for j in range(4):
                    pair = 4 * m + j
                    for b in range(2):
                        mm = pe.matmul(ps[S * b:S * b + S, OUT_BANK[l][t], 2 * DE * pair:2 * DE * (pair + 1)],
                                       probs_T[:, i % 2, P * j + S * b:P * j + S * b + S],
                                       v_pairs[l][:, t, b, pair, :], start=True, stop=True)
                mm.then_inc(pv_ready[l], 1)

            def transpose_output(T, l, *users):
                if idle(T, l):
                    return
                pe.wait_ge(o_ready[l], NT * (T - l + 1))
                bank_read(T, users)
                for t in range(NT):
                    for k in range(KT):
                        at = P * (KT * t + k)
                        mm = pe.transpose(ps[:, OUT_T_BANK[l], at:at + P], o_row[:, t, P * k:P * k + P],
                                          ident[:])
                mm.then_inc(oT_ready[l], 1)

            def output_product(T, l, *users):
                if idle(T, l):
                    return
                if first(T, l):
                    pe.wait_ge(w_lo_done, WCOL[f"o{l}"] // WBLK + 1)
                pe.wait_ge(o_lo_ready[l], T - l + 1)
                bank_read(T, users)
                for t in range(NT):
                    mm = split_product(ps[:, Y_BANK[l], D * t:D * t + D],
                                       [((o_hi[:, t, k, :], o_lo[:, t, k, :]), w_parts(f"o{l}", k, 0, D))
                                        for k in range(KT)], first=t == 0)
                mm.then_inc(y_ready[l], 1)

            def transpose_normed(T, n, *users):
                lag = (L0, FF)[n]
                if idle(T, lag):
                    return
                pe.wait_ge(xs_ready[n], T - lag + 1)
                bank_read(T, users)
                for k in range(KT):
                    for t in range(NT):
                        at = TC * k + P * t
                        mm = pe.transpose(ps[:, XS_T_BANK[n], at:at + P], xs_row[n][:, t, P * k:P * k + P],
                                          ident[:])
                mm.then_inc(xsT_ready[n], 1)

            def hidden_in(T, j, *users):
                if idle(T, FF):
                    return
                if first(T, FF) and j == 0:
                    pe.wait_ge(w_lo_done, NWB)
                if j == 0:
                    pe.wait_ge(ff_lo_ready, T - 1)
                bank_read(T, users)
                for n, name in enumerate(("gate", "hid")):
                    mm = split_product(ps[:, GU_BANK[j], TC * n:TC * n + TC],
                                       [(w_parts(name, k, P * j, P, HID), (ff_hi[:, k, :], ff_lo[:, k, :]))
                                        for k in range(KT)], first=n == 0)
                mm.then_inc(gu_ready, 1)

            def hidden_out(T, j, *users):
                if idle(T, FF):
                    return
                pe.wait_ge(h_lo_ready, NJ * (T - 2) + j + 1)
                bank_read(T, users)
                for t in range(NT):
                    rows = slice(P * t, P * t + P)
                    mm = split_product(ps[:, ACC_BANK, D * t:D * t + D],
                                       [((h_hi[:, j % 2, rows], h_lo[:, j % 2, rows]),
                                         w_parts("out", j, 0, D))],
                                       first=j == 0 and t == 0, last=j == NJ - 1)
                mm.then_inc(h_used, 1)

            def turn(T):
                project_keys(T, 1, (pT_copied[1], L1, NI, 4, BEFORE))
                project_queries(T, 1, (xs_g_ready[0], L0, 1, 1, BEFORE))
                project_values(T, 1, (o_ready[1], L1, NT, 2, BEFORE))
                transpose_normed(T, 1, (h_ready, FF, NJ, 8, BEFORE))
                project_keys(T, 0, (x2_ready, L1, 1, 1, BEFORE))
                project_queries(T, 0, (pT_copied[1], L1, NI, 2, BEFORE))
                project_values(T, 0, (k_copied[0], L0, 1, 1, NOW))
                hidden_in(T, 0, (xs_g_ready[1], FF, 1, 1, NOW))
                hidden_in(T, 1, (res_ready, FF, 1, 1, BEFORE))
                hidden_in(T, 2, (h_ready, FF, NJ, 7, BEFORE))
                hidden_in(T, 3, (h_ready, FF, NJ, 1, NOW))
                scores(T, 0, 0, (k_copied[1], L1, 1, 1, NOW))
                scores(T, 0, 1, (q_copied[1], L1, 1, 1, NOW))
                scores(T, 0, 2, (v_copied[1], L1, 1, 1, NOW))
                scores(T, 0, 3, (shifted_ready[0], L0, NI, 1, NOW))
                hidden_out(T, 0, (h_ready, FF, NJ, 2, NOW))
                transpose_probs(T, 0, 0, (q_copied[0], L0, 1, 1, NOW))
                transpose_probs(T, 0, 1, (v_copied[0], L0, 1, 1, NOW))
                scores(T, 1, 0, (shifted_ready[0], L0, NI, 2, NOW))
                transpose_probs(T, 0, 2, (shifted_ready[0], L0, NI, 3, NOW))
                weigh_values(T, 0, 0, (pT_copied[0], L0, NI, 1, NOW))
                weigh_values(T, 0, 1)
                transpose_probs(T, 0, 3, (shifted_ready[0], L0, NI, 4, NOW))
                scores(T, 1, 1, (pT_copied[0], L0, NI, 2, NOW))
                weigh_values(T, 0, 2, (pT_copied[0], L0, NI, 3, NOW))
                weigh_values(T, 0, 3)
                hidden_in(T, 4, (h_ready, FF, NJ, 3, NOW))
                transpose_output(T, 0, (pT_copied[0], L0, NI, 4, NOW))
                scores(T, 1, 2, (o_ready[0], L0, NT, 1, NOW))
                scores(T, 1, 3, (shifted_ready[1], L1, NI, 1, NOW))
                output_product(T, 0, (shifted_ready[1], L1, NI, 2, NOW))
                transpose_probs(T, 1, 0, (o_ready[0], L0, NT, 2, NOW))
                hidden_out(T, 1)
                transpose_probs(T, 1, 1, (shifted_ready[1], L1, NI, 3, NOW))
                hidden_in(T, 5, (h_ready, FF, NJ, 4, NOW))
                weigh_values(T, 1, 0, (shifted_ready[1], L1, NI, 4, NOW))
                transpose_probs(T, 1, 2, (pT_copied[1], L1, NI, 1, NOW))
                transpose_probs(T, 1, 3, (o_lo_ready[0], L0, 1, 1, NOW))
                weigh_values(T, 1, 1)
                weigh_values(T, 1, 2, (pT_copied[1], L1, NI, 3, NOW))
                hidden_out(T, 2)
                weigh_values(T, 1, 3)
                hidden_in(T, 6, (h_ready, FF, NJ, 5, NOW))
                hidden_out(T, 3)
                transpose_output(T, 1, (y_mod_ready, L0, 1, 1, NOW))
                hidden_out(T, 4)
                hidden_in(T, 7, (h_ready, FF, NJ, 6, NOW))
                transpose_normed(T, 0, (o_ready[1], L1, NT, 1, NOW))
                hidden_out(T, 5)
                output_product(T, 1, (o_lo_ready[1], L1, 1, 1, NOW))
                hidden_out(T, 6)
                hidden_out(T, 7)

            def first_turn(T):
                hidden_in(T, 0)
                hidden_out(T, 0)
                project_keys(T, 0, (y_mod_ready, L0, 1, 1, BEFORE))
                hidden_out(T, 1)
                hidden_in(T, 1)
                project_keys(T, 1, (o_lo_ready[0], L0, 1, 1, BEFORE))
                project_queries(T, 0, (o_ready[0], L0, NT, 1, BEFORE))
                project_values(T, 0, (k_copied[0], L0, 1, 1, NOW))
                modulations(T)
                hidden_in(T, 2)
                project_queries(T, 1, (xs_g_ready[0], L0, 1, 1, BEFORE))
                project_values(T, 1, (o_ready[0], L0, NT, 2, BEFORE))
                scores(T, 0, 0, (k_copied[1], L1, 1, 1, NOW))
                hidden_in(T, 3)
                hidden_in(T, 4)
                scores(T, 0, 1, (q_copied[1], L1, 1, 1, NOW))
                scores(T, 0, 2, (v_copied[1], L1, 1, 1, NOW))
                transpose_probs(T, 0, 0, (q_copied[0], L0, 1, 1, NOW))
                hidden_out(T, 2)
                scores(T, 0, 3, (shifted_ready[0], L0, NI, 1, NOW))
                scores(T, 1, 0, (shifted_ready[0], L0, NI, 2, NOW))
                transpose_probs(T, 0, 1, (v_copied[0], L0, 1, 1, NOW))
                weigh_values(T, 0, 0, (pT_copied[0], L0, NI, 1, NOW))
                transpose_probs(T, 0, 2, (shifted_ready[0], L0, NI, 3, NOW))
                weigh_values(T, 0, 1)
                transpose_probs(T, 0, 3, (shifted_ready[0], L0, NI, 4, NOW))
                scores(T, 1, 1, (pT_copied[0], L0, NI, 2, NOW))
                weigh_values(T, 0, 2, (pT_copied[0], L0, NI, 3, NOW))
                weigh_values(T, 0, 3)
                scores(T, 1, 2, (o_ready[0], L0, NT, 1, NOW))
                hidden_out(T, 3)
                transpose_probs(T, 1, 0, (o_ready[0], L0, NT, 2, NOW))
                transpose_output(T, 0, (pT_copied[0], L0, NI, 4, NOW))
                hidden_out(T, 4)
                scores(T, 1, 3, (shifted_ready[1], L1, NI, 1, NOW))
                hidden_in(T, 5)
                hidden_out(T, 5)
                output_product(T, 0, (pT_copied[0], L0, NI, 2, NOW), (shifted_ready[1], L1, NI, 2, NOW))
                weigh_values(T, 1, 0, (shifted_ready[1], L1, NI, 4, NOW))
                transpose_probs(T, 1, 1, (shifted_ready[1], L1, NI, 3, NOW))
                transpose_probs(T, 1, 2, (pT_copied[1], L1, NI, 1, NOW))
                transpose_probs(T, 1, 3, (o_lo_ready[0], L0, 1, 1, NOW))
                transpose_normed(T, 1)
                hidden_out(T, 6)
                weigh_values(T, 1, 1)
                weigh_values(T, 1, 2, (pT_copied[1], L1, NI, 3, NOW))
                weigh_values(T, 1, 3)
                transpose_output(T, 1, (y_mod_ready, L0, 1, 1, NOW))
                hidden_in(T, 6)
                transpose_normed(T, 0, (shifted_ready[0], L0, NI, 2, NOW), (o_ready[1], L1, NT, 1, NOW))
                output_product(T, 1, (o_lo_ready[1], L1, 1, 1, NOW))
                hidden_out(T, 7)
                hidden_in(T, 7)

            def last_turn(T):
                weigh_values(T, 0, 0)
                transpose_probs(T, 0, 0)
                scores(T, 0, 0)
                transpose_probs(T, 0, 1)
                scores(T, 0, 1)
                project_keys(T, 1, (pT_copied[1], L1, NI, 4, BEFORE))
                transpose_normed(T, 1, (h_ready, FF, NJ, 8, BEFORE))
                project_keys(T, 0)
                scores(T, 0, 2)
                transpose_probs(T, 0, 2)
                weigh_values(T, 0, 1)
                project_queries(T, 1, (xs_g_ready[0], L0, 1, 1, BEFORE))
                weigh_values(T, 0, 2)
                project_values(T, 1, (o_ready[1], L1, NT, 2, BEFORE))
                hidden_in(T, 0, (xs_g_ready[1], FF, 1, 1, NOW))
                output_product(T, 0)
                scores(T, 0, 3)
                hidden_in(T, 1, (res_ready, FF, 1, 1, BEFORE))
                scores(T, 1, 0, (q_copied[1], L1, 1, 1, NOW))
                hidden_in(T, 2, (h_ready, FF, NJ, 7, BEFORE))
                transpose_output(T, 0)
                hidden_in(T, 3, (h_ready, FF, NJ, 1, NOW))
                hidden_out(T, 0, (h_ready, FF, NJ, 2, NOW))
                scores(T, 1, 1, (x2_ready, L1, 1, 1, BEFORE))
                scores(T, 1, 2, (pT_copied[1], L1, NI, 2, BEFORE))
                weigh_values(T, 0, 3)
                scores(T, 1, 3, (shifted_ready[1], L1, NI, 1, NOW))
                hidden_out(T, 1)
                hidden_in(T, 4, (h_ready, FF, NJ, 3, NOW))
                transpose_probs(T, 0, 3)
                transpose_probs(T, 1, 0, (v_copied[1], L1, 1, 1, NOW))
                hidden_in(T, 5, (h_ready, FF, NJ, 4, NOW))
                transpose_probs(T, 1, 1, (shifted_ready[1], L1, NI, 3, NOW))
                weigh_values(T, 1, 0, (shifted_ready[1], L1, NI, 4, NOW))
                project_queries(T, 0)
                transpose_probs(T, 1, 2, (pT_copied[1], L1, NI, 1, NOW))
                weigh_values(T, 1, 1)
                transpose_normed(T, 0)
                transpose_probs(T, 1, 3, (k_copied[1], L1, 1, 1, NOW))
                hidden_out(T, 2)
                weigh_values(T, 1, 2, (pT_copied[1], L1, NI, 3, NOW))
                weigh_values(T, 1, 3)
                hidden_in(T, 6, (h_ready, FF, NJ, 5, NOW))
                transpose_output(T, 1, (shifted_ready[1], L1, NI, 2, NOW))
                hidden_out(T, 3)
                hidden_in(T, 7, (h_ready, FF, NJ, 6, NOW))
                output_product(T, 1, (o_lo_ready[1], L1, 1, 1, NOW))
                hidden_out(T, 4)
                hidden_out(T, 5)
                hidden_out(T, 6)
                hidden_out(T, 7)
                project_values(T, 0)

            first_turn(0)
            first_turn(1)
            pe.wait_ge(modT_done, 1)
            turn(2)
            with pe.Fori(3, NCH) as T:
                turn(T)
            last_turn(NCH)
            last_turn(NCH + 1)


def kernel(**inputs):
    import numpy as np
    import concourse.bacc as bacc
    from concourse.bass_utils import run_bass_kernel_spmd

    def T(name):
        return np.asarray(inputs[name]).T

    def tiles(w):
        return w.reshape(-1, P, w.shape[1]).transpose(1, 0, 2).reshape(P, -1)

    def cols(name):
        return np.asarray(inputs[name]).reshape(KT, P).T

    names = ["L0_cond_Wk", "L0_cond_Wq", "L0_cond_Wv", "L0_cond_Wo", "L1_cond_Wk", "L1_cond_Wq",
             "L1_cond_Wv", "L1_cond_Wo", "L1_cond_gate_w", "L1_cond_hid_w", "L1_cond_out_w"]
    x = np.asarray(inputs["x"]).reshape(NCH, NT, P, D)
    arrays = {
        "x": x,
        "xT": x.reshape(NCH, TC, KT, P).transpose(0, 3, 2, 1),
        "weights": np.concatenate([tiles(T(n)) for n in names], axis=1),
        "condT": T("cond_256"),
        "wcT": T("L0_cond_Wc"),
        "bc": np.asarray(inputs["L0_cond_bc"]),
        "rms": np.asarray(inputs["L0_cond_rms_scale"]),
        "g1wT": T("L1_cond_g1w"), "b1wT": T("L1_cond_b1w"),
        "g2wT": T("L1_cond_g2w"), "b2wT": T("L1_cond_b2w"),
        "modb": np.concatenate([cols("L1_cond_" + n) for n in ("g1b", "b1b", "g2b", "b2b")], axis=1),
        "mask": np.asarray(inputs["mask_SxS_bk1"]),
    }
    arrays = {n: np.ascontiguousarray(v) for n, v in arrays.items()}

    nc = bacc.Bacc("TRN2", target_bir_lowering=False, num_devices=1)
    aps = {n: nc.dram_tensor(f"in_{n}", v.shape, mybir.dt.from_np(v.dtype), kind="ExternalInput").ap()
           for n, v in arrays.items()}
    out = nc.dram_tensor("out", (NCH, NT, P, D), F32, kind="ExternalOutput").ap()
    build(nc, aps, out)
    r = run_bass_kernel_spmd(nc, [{f"in_{n}": v for n, v in arrays.items()}], core_ids=[0])
    return r.results[0]["out"].reshape(NB, S, D)
```
